# Optimizing a Trainium2 kernel written in Bass

```python
import numpy as np
import jax
import jax.numpy as jnp

def _softmax(x, axis=-1):
    return jax.nn.softmax(x, axis=axis)

def _gelu(x):
    return jax.nn.gelu(x, approximate=True)

def _silu(x):
    return jax.nn.silu(x)

def _sigmoid(x):
    return jax.nn.sigmoid(x)

def _layernorm(x, axis=-1, eps=1e-05):
    m = jnp.mean(x, axis=axis, keepdims=True)
    v = jnp.var(x, axis=axis, keepdims=True)
    return (x - m) / jnp.sqrt(v + eps)

def _scatter_add(tgt, idx, src, axis=0):
    return tgt.at[idx].add(src)

def _segment_sum(src, seg, n):
    return jax.ops.segment_sum(src, seg, n)
kernel_name = 'mk_adj_resnorm_d1_adj_r2_5f6a17'

def setup_inputs(seed: int=0):
    np.random.seed(seed)
    _w = jnp.asarray

    def _rec_inputs():
        import jax
        import jax.numpy as jnp
        _gk = jax.random.key(seed)
        x = -9.806e-05 + 1 * jax.random.normal(jax.random.fold_in(_gk, 1), (2048, 128), jnp.float32)
        _a = jax.random.bernoulli(jax.random.fold_in(_gk, 2), 0.00195312, (2048, 2048))
        _a = jnp.logical_or(_a, jnp.swapaxes(_a, -1, -2))
        _a = jnp.logical_or(_a, jnp.eye(2048, dtype=bool))
        _af = _a.astype(jnp.float32)
        _af = _af * jax.random.uniform(jax.random.fold_in(_gk, 3), (2048, 2048), jnp.float32, 0.05, 1)
        adj = _af
        return (x, adj)
    x, adj = _rec_inputs()

    def _L0_gnn_setup():
        import jax, jax.numpy as jnp
        import numpy as np
        N_NODE = 2048
        N_FEA_IN = 128
        N_FEA_OUT = 128
        key = jax.random.key(seed)
        k_x, k_a, k_w, k_att = jax.random.split(key, 4)
        stdv_w = 1.0 / np.sqrt(N_FEA_OUT)
        stdv_a = 1.0 / np.sqrt(2 * N_FEA_OUT)
        X = jax.random.normal(k_x, (N_NODE, N_FEA_IN), dtype=jnp.float32)
        A = jax.random.uniform(k_a, (N_NODE, N_NODE), dtype=jnp.float32)
        W = jax.random.uniform(k_w, (N_FEA_IN, N_FEA_OUT), minval=-stdv_w, maxval=stdv_w, dtype=jnp.float32)
        a = jax.random.uniform(k_att, (1, 2 * N_FEA_OUT), minval=-stdv_a, maxval=stdv_a, dtype=jnp.float32)
        return {'X': X, 'A': A, 'W': W, 'a': a}
    _L0_gnn_all = _L0_gnn_setup()
    _L0_gnn_in = {k: v for k, v in _L0_gnn_all.items() if k in ('W', 'a')}
    del _L0_gnn_all
    return {'x': x, 'adj': adj, 'L0_gnn_W': _L0_gnn_in['W'], 'L0_gnn_a': _L0_gnn_in['a']}

def reference(x, adj, L0_gnn_W, L0_gnn_a):
    import jax
    import jax.numpy as jnp

    def _L0_gnn_ref(X, A, W, a):
        import jax, jax.numpy as jnp
        import numpy as np
        N_NODE = 2048
        N_FEA_IN = 128
        N_FEA_OUT = 128
        XW = jnp.matmul(X, W)
        f = W.shape[1]
        s_col = jnp.matmul(XW, a[0, :f])
        s_row = jnp.matmul(XW, a[0, f:])
        Z1 = jax.nn.leaky_relu(s_row[:, None] + s_col[None, :], negative_slope=0.01)
        den = jnp.exp(Z1)
        num = jnp.matmul(A, den)
        att = jnp.where(num != 0, den / jnp.where(num != 0, num, 1.0), 0.0)
        H = jnp.matmul(A, jnp.matmul(att, XW))
        return H
    x = _layernorm(x + _L0_gnn_ref(x, adj, L0_gnn_W, L0_gnn_a), axis=-1)
    return x

_drawn_inputs = setup_inputs


def setup_inputs(seed=0):
    import zlib

    import numpy as np

    out = dict(_drawn_inputs(seed))
    spreads = {}
    factors = {}
    for name, (base, spread) in spreads.items():
        noise = np.random.default_rng([zlib.crc32(name.encode()), seed]).standard_normal(out[name].shape)
        drawn = base * np.exp(spread * noise) if base else spread * noise
        out[name] = jnp.asarray(drawn.astype(out[name].dtype))
    for name, factor in factors.items():
        out[name] = (out[name] * factor).astype(out[name].dtype)
    return out
```

```python
import concourse.bass as bass
from concourse import mybir
from contextlib import ExitStack

P = 128
W = 512
FEAT = 128


def graph_attention_layernorm(nc, xT, x, adjT, w, a2, out):
    F32 = mybir.dt.float32
    ALU = mybir.AluOpType
    ACT = mybir.ActivationFunctionType
    N = x.shape[0]
    NB = N // P
    NC = N // W
    NP2 = NB // 2
    SLOPE = 0.01
    EPS = 1e-5

    ctx = ExitStack()
    with ctx:
        def sb(name, shape):
            return ctx.enter_context(nc.sbuf_tensor(name, shape, F32))

        def sem(name):
            return ctx.enter_context(nc.semaphore(name))

        AT = sb("AT", [P, NB, N])
        den0 = sb("den0", [P, NB, P])
        den1 = sb("den1", [P, NB, P])
        den = [den0, den1]
        rrow = sb("rrow", [P, N])
        crow = sb("crow", [P, N])
        xw = sb("xw", [P, NB, FEAT])
        xTs = sb("xTs", [P, N])
        att = sb("att", [P, 2, W])
        zt = sb("zt", [P, W])
        dn = sb("dn", [P, 2, W])
        safe = sb("safe", [P, W])
        xwp = sb("xwp", [P, 2, FEAT])
        ws = sb("ws", [P, FEAT])
        a2s = sb("a2s", [P, 2])
        acs = sb("acs", [P, 2, P])
        ones = sb("ones", [P, P])
        ident = sb("ident", [P, P])
        rc = sb("rc", [P, NB, 2])
        epst = sb("epst", [P, 1])
        stats = sb("stats", [P, NB, 6])
        mv = sb("mv", [P, NB, 2])
        rstd = sb("rstd", [P, NB])

        xwT = den1[:, :, :].rearrange("p b j -> p (b j)")
        BT = xTs
        B = den0
        HT = crow
        xs = den1
        y = xw

        ps = ctx.enter_context(nc.psum_tensor("ps", [P, 8, W], F32))
        num = [ps[:, c, :] for c in range(NC)]
        bt = [ps[:, NC + c, :] for c in range(NC)]

        s_in = sem("inputs_loaded")
        s_at = sem("adj_loaded")
        s_x = sem("x_loaded")
        s_pool = sem("constants_set")
        s_acs = sem("a_spread")
        s_p0 = sem("setup_products")
        s_e0 = sem("setup_evicted")
        s_lz = sem("den_exponent_ready")
        s_xwp = sem("xwp_ready")
        s_den = sem("den_ready")
        s_num = sem("num_ready")
        s_dz = sem("att_exponent_ready")
        s_dn = sem("att_den_ready")
        s_att = sem("att_ready")
        s_bt = sem("bt_added")
        s_v = sem("vector_steps")
        s_bts = sem("bt_evicted")
        s_tb = sem("b_transposed")
        s_bs = sem("b_evicted")
        s_ht = sem("ht_ready")
        s_hts = sem("ht_evicted")
        s_th = sem("h_transposed")
        s_var = sem("variances_ready")
        s_std = sem("std_ready")
        s_y = sem("y_ready")
        s_out = sem("stored")
        block = ctx.enter_context(nc.Block())

        PER_CHUNK = 5
        PER_BLOCK = NC * PER_CHUNK + 1

        def before(J, c):
            return J * PER_BLOCK + 1 + c * PER_CHUNK + (c > 0)

        def masked(J, c):
            return before(J, c) + PER_CHUNK

        @block.sync
        def _(sp):
            sp.dma_start(xTs[:, :], xT).then_inc(s_in, 16)
            sp.dma_start(ws[:, :], w).then_inc(s_in, 16)
            sp.dma_start(a2s[:, :], a2).then_inc(s_in, 16)
            for b in range(NB):
                sp.dma_start(AT[:, b, :], adjT[b * P:(b + 1) * P, :]).then_inc(s_at, 16)
            sp.wait_ge(s_num, NB * NC)
            sp.dma_start(xs[:, :, :], x.rearrange("(b p) f -> p b f", p=P)).then_inc(s_x, 16)
            for h in range(2):
                sp.wait_ge(s_y, h + 1)
                sp.dma_start(out.rearrange("(b p) f -> p b f", p=P)[:, h * 8:(h + 1) * 8, :],
                             y[:, h * 8:(h + 1) * 8, :]).then_inc(s_out, 16)
            sp.wait_ge(s_out, 32)

        @block.gpsimd
        def _(pool):
            nc.gpsimd.memset(ones[:, :], 1.0).then_inc(s_pool, 1)
            nc.gpsimd.memset(epst[:, :], EPS).then_inc(s_pool, 1)
            pool.wait_ge(s_pool, 2)
            nc.gpsimd.affine_select(out=ident[:, :], in_=ones[:, :], compare_op=ALU.is_equal, fill=0.0, base=0,
                                    pattern=[[-1, P]], channel_multiplier=1).then_inc(s_pool, 1)

        @block.tensor
        def _(pe):
            pe.wait_ge(s_in, 48)
            for c in range(NC):
                mm = nc.tensor.matmul(num[c], ws[:, :], xTs[:, c * W:(c + 1) * W], start=True, stop=True)
            mm.then_inc(s_p0, 1)
            for b in range(NB):
                mm = nc.tensor.matmul(bt[b // 4][:, (b % 4) * P:(b % 4 + 1) * P], xTs[:, b * P:(b + 1) * P], ws[:, :],
                                      start=True, stop=True)
            mm.then_inc(s_p0, 1)
            pe.wait_ge(s_e0, 1)
            pe.wait_ge(s_acs, 2)
            for c in range(NC):
                mm = nc.tensor.matmul(num[c], acs[:, 1, :], xwT[:, c * W:(c + 1) * W], start=True, stop=True)
            mm.then_inc(s_p0, 1)
            pe.wait_ge(s_e0, 2)
            for c in range(NC):
                mm = nc.tensor.matmul(bt[c], acs[:, 0, :], xwT[:, c * W:(c + 1) * W], start=True, stop=True)
            mm.then_inc(s_p0, 1)
            pe.wait_ge(s_e0, 3)
            for b in range(NB):
                mm = nc.tensor.matmul(num[0][:, 2 * b:2 * b + 2], xwT[:, b * P:(b + 1) * P], a2s[:, :],
                                      start=True, stop=True)
            mm.then_inc(s_p0, 1)
            pe.wait_ge(s_e0, 5)
            pe.wait_ge(s_at, 16 * NB)

            def add_bt(J, pu, c, t, first, last):
                if c == 0:
                    pe.wait_ge(s_xwp, J + 1)
                pe.wait_ge(s_att, t + 1)
                nc.tensor.matmul(bt[c], xwp[:, pu, :], att[:, c % 2, :],
                                 start=first, stop=last).then_inc(s_bt, 1)

            def pair(J0, first, last):
                for u in range(2):
                    pe.wait_ge(s_den, J0 + u + 1)
                    for c in range(NC):
                        t = (J0 + u) * NC + c
                        if not (first and u == 0):
                            pe.wait_ge(s_v, masked(J0 + u - 1, c))
                        for k in range(NB):
                            mm = nc.tensor.matmul(num[c], den[u][:, k, :], AT[:, k, c * W:(c + 1) * W],
                                                  start=(k == 0), stop=(k == NB - 1))
                        mm.then_inc(s_num, 1)
                        if not (first and u == 0 and c == 0):
                            pu, pc = (u, c - 1) if c else (u - 1, NC - 1)
                            add_bt(J0 + pu, pu % 2, pc, t - 1, first and pu == 0, last and pu == 1)

            pair(0, True, False)
            with pe.Fori(1, NP2 - 1) as p:
                pair(2 * p, False, False)
            pair(NB - 2, False, True)
            add_bt(NB - 1, 1, NC - 1, NB * NC - 1, False, True)

            pe.wait_ge(s_pool, 3)
            pe.wait_ge(s_bts, 1)
            for b in range(NB):
                mm = nc.tensor.transpose(num[b // 4][:, (b % 4) * P:(b % 4 + 1) * P], BT[:, b * P:(b + 1) * P], ident[:, :])
            mm.then_inc(s_tb, 1)
            pe.wait_ge(s_bs, 1)
            for c in range(NC):
                for k in range(NB):
                    mm = nc.tensor.matmul(bt[c], B[:, k, :], AT[:, k, c * W:(c + 1) * W], start=(k == 0), stop=(k == NB - 1))
                mm.then_inc(s_ht, 1)
            for c in range(NC):
                pe.wait_ge(s_hts, c + 1)
                for b in range(4 * c, 4 * c + 4):
                    mm = nc.tensor.transpose(num[c][:, (b % 4) * P:(b % 4 + 1) * P], HT[:, b * P:(b + 1) * P], ident[:, :])
                mm.then_inc(s_th, 1)

        @block.scalar
        def _(act):
            act.wait_ge(s_p0, 1)
            nc.scalar.activation(xwT[:, :], ps[:, 0:4, :].rearrange("p c w -> p (c w)"), ACT.Identity).then_inc(s_e0, 1)
            act.wait_ge(s_p0, 2)
            act.wait_ge(s_e0, 1)
            nc.scalar.activation(xw[:, :, :].rearrange("p b f -> p (b f)"),
                                 ps[:, 4:8, :].rearrange("p c w -> p (c w)"), ACT.Identity).then_inc(s_e0, 1)

            def exps(J, u, first=False):
                if not first:
                    act.wait_ge(s_bt, (J - 1) * NC)
                nc.scalar.copy(xwp[:, u, :], xw[:, bass.ds(J, 1), :]).then_inc(s_xwp, 1)
                act.wait_ge(s_lz, J + 1)
                nc.scalar.activation(den[u][:, :, :], den[u][:, :, :], ACT.Exp).then_inc(s_den, 1)

            act.wait_ge(s_e0, 2)
            exps(0, 0, True)

            def pair(J0, first, last):
                for u in range(2):
                    for c in range(NC):
                        t = (J0 + u) * NC + c
                        act.wait_ge(s_dz, t + 1)
                        nc.scalar.activation(dn[:, c % 2, :], dn[:, c % 2, :], ACT.Exp).then_inc(s_dn, 1)
                        if c == 0 and not (last and u == 1):
                            exps(J0 + u + 1, 1 - u, first and u == 0)

            pair(0, True, False)
            with act.Fori(1, NP2 - 1) as p:
                pair(2 * p, False, False)
            pair(NB - 2, False, True)
            act.wait_ge(s_bt, NB * NC)
            nc.scalar.activation(BT[:, :], ps[:, 4:8, :].rearrange("p c w -> p (c w)"), ACT.Identity).then_inc(s_bts, 1)
            act.wait_ge(s_tb, 1)
            nc.scalar.activation(B[:, :, :].rearrange("p b f -> p (b f)"),
                                 ps[:, 0:4, :].rearrange("p c w -> p (c w)"), ACT.Identity).then_inc(s_bs, 1)
            for c in range(NC):
                act.wait_ge(s_ht, c + 1)
                nc.scalar.activation(HT[:, c * W:(c + 1) * W], bt[c], ACT.Identity).then_inc(s_hts, 1)
            act.wait_ge(s_var, 1)
            nc.scalar.activation(rstd[:, :], mv[:, :, 1], ACT.Sqrt, bias=epst[:, :]).then_inc(s_std, 1)

        @block.vector
        def _(dve):
            dve.wait_ge(s_pool, 2)
            dve.wait_ge(s_in, 48)
            for h in range(2):
                nc.vector.tensor_scalar(acs[:, h, :], ones[:, :], a2s[:, h:h + 1], None, ALU.mult).then_inc(s_acs, 1)
            dve.wait_ge(s_e0, 2)
            dve.wait_ge(s_p0, 3)
            nc.vector.tensor_copy(rrow[:, :], ps[:, 0:4, :].rearrange("p c w -> p (c w)")).then_inc(s_e0, 1)
            dve.wait_ge(s_p0, 4)
            nc.vector.tensor_copy(crow[:, :], ps[:, 4:8, :].rearrange("p c w -> p (c w)")).then_inc(s_e0, 1)
            dve.wait_ge(s_p0, 5)
            nc.vector.tensor_copy(rc[:, :, :].rearrange("p b t -> p (b t)"), ps[:, 0, 0:2 * NB]).then_inc(s_e0, 1)
            dve.wait_ge(s_e0, 5)

            def exponent(J, u, v):
                flat = den[u][:, :, :].rearrange("p b j -> p (b j)")
                for k in range(NB):
                    i = nc.vector.tensor_scalar(den[u][:, k, :], crow[:, bass.ds(J * P, P)], rc[:, k, 1:2], None, ALU.add)
                i.then_inc(s_v, 1)
                dve.wait_ge(s_v, v + 1)
                nc.vector.scalar_tensor_tensor(flat, flat, SLOPE, flat, ALU.mult, ALU.max).then_inc(s_lz, 1)

            exponent(0, 0, 0)

            def pair(J0, first, last):
                for u in range(2):
                    J = J0 + u
                    for c in range(NC):
                        t = J * NC + c
                        q = c % 2
                        cs = slice(c * W, (c + 1) * W)
                        v = before(J, c) - (last and u == 1 and c > 0)
                        nc.vector.tensor_scalar(zt[:, :], rrow[:, cs], rc[:, bass.ds(J, 1), 0], None, ALU.add).then_inc(s_v, 1)
                        dve.wait_ge(s_v, v + 1)
                        if not (first and u == 0 and c == 0):
                            dve.wait_ge(s_att, t)
                        nc.vector.scalar_tensor_tensor(dn[:, q, :], zt[:, :], SLOPE, zt[:, :],
                                                       ALU.mult, ALU.max).then_inc(s_dz, 1)
                        dve.wait_ge(s_dz, t + 1)
                        dve.wait_ge(s_num, t + 1)
                        nc.vector.tensor_scalar(zt[:, :], num[c], 0.0, None, ALU.is_equal).then_inc(s_v, 1)
                        dve.wait_ge(s_v, v + 2)
                        nc.vector.tensor_tensor(safe[:, :], zt[:, :], num[c], ALU.add).then_inc(s_v, 1)
                        dve.wait_ge(s_v, v + 3)
                        nc.vector.reciprocal(safe[:, :], safe[:, :]).then_inc(s_v, 1)
                        dve.wait_ge(s_dn, t + 1)
                        nc.vector.scalar_tensor_tensor(dn[:, q, :], num[c], 0.0, dn[:, q, :],
                                                       ALU.not_equal, ALU.mult).then_inc(s_v, 1)
                        dve.wait_ge(s_v, v + 5)
                        if not (first and u == 0 and c < 2):
                            dve.wait_ge(s_bt, t - 1)
                        nc.vector.tensor_tensor(att[:, q, :], dn[:, q, :], safe[:, :], ALU.mult).then_inc(s_att, 1)
                        if c == 0 and not (last and u == 1):
                            exponent(J + 1, 1 - u, v + PER_CHUNK)

            pair(0, True, False)
            with dve.Fori(1, NP2 - 1) as p:
                pair(2 * p, False, False)
            pair(NB - 2, False, True)

            dve.wait_ge(s_x, 16)
            v = 1 + NB * PER_BLOCK - 1
            for c in range(NC):
                dve.wait_ge(s_th, c + 1)
                for b in range(4 * c, 4 * c + 4):
                    nc.vector.tensor_tensor(y[:, b, :], xs[:, b, :], num[c][:, (b % 4) * P:(b % 4 + 1) * P],
                                            ALU.add).then_inc(s_v, 1)
                    v += 1
                    dve.wait_ge(s_v, v)
                    nc.vector.bn_stats(stats[:, b, :], y[:, b, :]).then_inc(s_v, 1)
                    v += 1
                    dve.wait_ge(s_v, v)
                    i = nc.vector.bn_aggr(mv[:, b, :], stats[:, b, :])
            i.then_inc(s_var, 1)
            dve.wait_ge(s_std, 1)
            nc.vector.reciprocal(rstd[:, :], rstd[:, :]).then_inc(s_v, 1)
            dve.wait_ge(s_v, v + 1)
            for b in range(NB):
                i = nc.vector.tensor_scalar(y[:, b, :], y[:, b, :], mv[:, b, 0:1], rstd[:, b:b + 1],
                                            ALU.subtract, ALU.mult)
                if b % 8 == 7:
                    i.then_inc(s_y, 1)


def kernel(x, adj, L0_gnn_W, L0_gnn_a):
    import numpy as np
    import concourse.bacc as bacc
    from concourse import mybir
    from concourse.bass_utils import run_bass_kernel_spmd

    a = np.asarray(L0_gnn_a)
    x = np.asarray(x)
    arrays = {
        "xT": np.ascontiguousarray(x.T),
        "x": np.ascontiguousarray(x),
        "adjT": np.ascontiguousarray(np.asarray(adj).T),
        "w": np.ascontiguousarray(L0_gnn_W),
        "a2": np.ascontiguousarray(a.reshape(2, FEAT).T),
    }
    nc = bacc.Bacc("TRN2", target_bir_lowering=False, num_devices=1)
    args = [nc.dram_tensor(n, v.shape, mybir.dt.from_np(v.dtype), kind="ExternalInput").ap() for n, v in arrays.items()]
    args.append(nc.dram_tensor("out", x.shape, mybir.dt.float32, kind="ExternalOutput").ap())
    graph_attention_layernorm(nc, *args)
    r = run_bass_kernel_spmd(nc, [arrays], core_ids=[0])
    return r.results[0]["out"]
```

```python
import concourse.bass as bass
from concourse import mybir
from contextlib import ExitStack
import numpy as np

P = 128
W = 512
FEAT = 128
SLOPE = 0.01
EPS = 1e-5
TINY = 1e-18
NODES = 2048
NB = NODES // P
NS = 2 * NB - 1
BATCH = ((0, NB), (NB, NS))
R = 96
DSCALE = 8 * float(np.log(2.0))


def constants():
    q = np.arange(P)
    b = (q % 32) // NB
    cols = [np.where(b == 0, 1.0, SLOPE), np.where(b == 0, q % NB, -(q % NB)), 1.0 - b, -1.0 * b]
    rows = np.concatenate([np.arange(NB) + NB - 1.0, np.arange(NS) * 1.0])
    cst = np.concatenate([np.stack(cols, 1), np.broadcast_to(rows, (P, rows.size))], 1).astype(np.float32)
    before = (q[None, :] < q[:, None]).astype(np.float32)
    k = np.arange(NODES).reshape(NB, P).T
    ids = np.stack([2 * k, 2 * k + 1, k, k], 2).astype(np.int32)
    return cst, before, ids


def graph_attention_layernorm(nc, xT, x, adjT, w, wT, a2, cst, before, ids, out):
    F32 = mybir.dt.float32
    F16 = mybir.dt.float16
    I32 = mybir.dt.int32
    U32 = mybir.dt.uint32
    ALU = mybir.AluOpType
    ACT = mybir.ActivationFunctionType
    AX = mybir.AxisListType
    N = NODES
    NC = N // W
    NP2 = NB // 2
    H = N // 2
    NG = 3

    ctx = ExitStack()
    with ctx:
        def sb(name, shape, dt=F32):
            return ctx.enter_context(nc.sbuf_tensor(name, shape, dt))

        def sem(name):
            return ctx.enter_context(nc.semaphore(name))

        def dram(name, shape, dt=F32):
            return nc.dram_tensor(name, shape, dt, kind="Internal").ap()

        Ahi = sb("Ahi", [P, NB, N], F16)
        Alo = sb("Alo", [P, NB, N], F16)
        stage = sb("stage", [P, NG * H])
        rrow = sb("rrow", [P, N])
        crow = sb("crow", [P, N])
        D = sb("D", [P, 2, NS, P], F16)
        xws = sb("xws", [P, N])
        wgt = sb("wgt", [P, N], F16)
        sums = sb("sums", [P, N], F16)
        E = sb("E", [P, 2, NB, R], F16)
        rcol = sb("rcol", [P, NB])
        ccol = sb("ccol", [P, NB])
        rs = sb("rs", [P, NB])
        cs = sb("cs", [P, NB])
        cnt = sb("cnt", [P, 2, 3, NB])
        rank = sb("rank", [P, 2, NB], U32)
        perm = sb("perm", [P, 2, NB, 4], I32)
        idt = sb("idt", [P, NB, 4], I32)
        cstt = sb("cstt", [P, 4 + NB + NS])
        tri = sb("tri", [P, P])
        ident = sb("ident", [P, P])
        wTs = sb("wTs", [P, FEAT])
        ws = sb("ws", [P, FEAT])
        a2s = sb("a2s", [P, 2])
        wa = sb("wa", [P, 2])
        xwp = sb("xwp", [P, 2, FEAT])
        ends = sb("ends", [P, 2, NB])
        sc = sb("sc", [P, 8])
        t16 = sb("t16", [P, 4, NB])
        eexp = sb("eexp", [P, 2, NB])
        steps = sb("steps", [P, 2, NS])
        lohi = sb("lohi", [P, 2, NB], I32)
        jk = sb("jk", [P, 2, NS], I32)
        mask = sb("mask", [P, NB])
        epst = sb("epst", [P, 2])
        stats = sb("stats", [P, NB, 6])
        mv = sb("mv", [P, NB, 2])
        rstd = sb("rstd", [P, NB])
        cj = sb("cj", [P, 2])
        z16 = sb("z16", [P, P], F16)

        xTs = xws
        srow = stage[0:2, 0:N]
        junk = D[:, :, :, :].rearrange("p a s j -> p (a s j)")[:, 0:N]
        st = [stage[:, g * H:(g + 1) * H] for g in range(NG)]
        tmp = xws
        q_t = [crow[:, 0:W], crow[:, W:2 * W]]
        lz_t = [crow[:, 2 * W:3 * W], crow[:, 3 * W:4 * W]]
        L_t = [stage[:, 0:W], stage[:, W:2 * W]]
        att = [stage[:, (2 + i) * W:(3 + i) * W] for i in range(4)]
        BT = rrow
        Bn = crow
        Bs = xws
        B16 = D[:, :, 0:NB, :]
        HT = rrow
        xs = stage[:, 0:N]
        y = crow[:, :].rearrange("p (b f) -> p b f", b=NB)

        d_rows = dram("d_rows", [2, N])
        d_xw = dram("d_xw", [N, FEAT])
        d_perm = [dram(f"d_perm{i}", [N, 4], I32) for i in range(2)]
        d_val = [dram(f"d_val{i}", [N, 1]) for i in range(2)]
        d_b = dram("d_b", [N, FEAT])

        ps = ctx.enter_context(nc.psum_tensor("ps", [P, 8, W], F32))
        num = [ps[:, c, :] for c in range(NC)]
        bt = [ps[:, NC + c, :] for c in range(NC)]

        names = """in_w in_x in_c p_wa wa_sb p_rows rows_sb rows_out row_r row_c cols_in p_xw xw_sb xw_out const
            rank_r rank_c sc_r sc_c val_r val_c perm_r perm_c rs_in cs_in ends_in crow_in
            g0 g1 g2 hi_done lo_done e_zero e_ready p_sums sums_hi sums_sb m_ready e_exp v jk_ready d_z d_lz d_exp d_hi d_lo
            w_exp w_m w_hi w_lo xws_in
            cj_ready num_ready q_ready lz_ready sq_done ln_done sub_done exp_done att_ready bt_added xwp_ready
            bt_sb b_t b_sb b_out b_in bhi_done blo_done ht ht_sb h_t x_in var std y_ready stored""".split()
        S = {n: sem(n) for n in names}
        block = ctx.enter_context(nc.Block())

        @block.sync
        def _(sp):
            sp.dma_start(wTs[:, :], wT).then_inc(S["in_w"], 16)
            sp.dma_start(a2s[:, :], a2).then_inc(S["in_w"], 16)
            sp.dma_start(xTs[:, :], xT).then_inc(S["in_x"], 16)
            sp.dma_start(ws[:, :], w).then_inc(S["in_x"], 16)
            sp.dma_start(tri[:, :], before).then_inc(S["in_c"], 16)
            sp.dma_start(idt[:, :, :], ids).then_inc(S["in_c"], 16)
            sp.dma_start(cstt[:, :], cst).then_inc(S["in_c"], 16)
            sp.wait_ge(S["rows_sb"], 1)
            sp.dma_start(d_rows, srow).then_inc(S["rows_out"], 16)
            sp.wait_ge(S["rows_out"], 16)
            sp.dma_start(rcol[:, :], d_rows[1].rearrange("(b p) -> p b", p=P), allow_slow_non_contiguous=True).then_inc(S["row_r"], 16)
            sp.dma_start(rrow[:, :], d_rows[1:2, :].to_broadcast([P, N])).then_inc(S["row_r"], 16)
            sp.dma_start(ccol[:, :], d_rows[0].rearrange("(b p) -> p b", p=P), allow_slow_non_contiguous=True).then_inc(S["row_c"], 16)
            sp.dma_start(crow[:, :], d_rows[0:1, :].to_broadcast([P, N])).then_inc(S["row_c"], 16)
            sp.wait_ge(S["xw_sb"], 1)
            sp.dma_start(d_xw.rearrange("(b p) f -> p b f", p=P), stage[:, 0:N].rearrange("p (b f) -> p b f", b=NB)
                         ).then_inc(S["xw_out"], 16)
            sp.wait_ge(S["sc_r"], 16 * NB)
            sp.dma_start(perm[:, 0, :, :], d_perm[0].rearrange("(b p) t -> p b t", p=P)).then_inc(S["perm_r"], 16)
            sp.wait_ge(S["val_r"], 16 * NB)
            sp.dma_start(rs[:, :], d_val[0].rearrange("(b p) o -> p (b o)", p=P), allow_slow_non_contiguous=True).then_inc(S["rs_in"], 16)
            byblock = d_val[0].rearrange("(b p) o -> p (b o)", p=P)
            sp.dma_start(ends[:, 0, :], byblock[0:1, :].to_broadcast([P, NB]), allow_slow_non_contiguous=True).then_inc(S["ends_in"], 16)
            sp.dma_start(ends[:, 1, :], byblock[P - 1:P, :].to_broadcast([P, NB]), allow_slow_non_contiguous=True).then_inc(S["ends_in"], 16)
            sp.wait_ge(S["sc_c"], 16 * NB)
            sp.dma_start(perm[:, 1, :, :], d_perm[1].rearrange("(b p) t -> p b t", p=P)).then_inc(S["perm_c"], 16)
            sp.wait_ge(S["val_c"], 16 * NB)
            sp.wait_ge(S["rank_c"], 4)
            sp.dma_start(crow[:, :], d_val[1].rearrange("n o -> o n").to_broadcast([P, N])).then_inc(S["crow_in"], 16)
            sp.dma_start(cs[:, :], d_val[1].rearrange("(b p) o -> p (b o)", p=P), allow_slow_non_contiguous=True).then_inc(S["cs_in"], 16)
            sp.wait_ge(S["b_sb"], 1)
            sp.dma_start(d_b.rearrange("(b p) f -> p b f", p=P), Bn[:, :].rearrange("p (b f) -> p b f", b=NB)
                         ).then_inc(S["b_out"], 16)
            sp.dma_start(xs.rearrange("p (b f) -> p b f", b=NB), x.rearrange("(b p) f -> p b f", p=P)).then_inc(S["x_in"], 16)
            for h in range(2):
                sp.wait_ge(S["y_ready"], h + 1)
                sp.dma_start(out.rearrange("(b p) f -> p b f", p=P)[:, h * 8:(h + 1) * 8, :],
                             y[:, h * 8:(h + 1) * 8, :]).then_inc(S["stored"], 16)
            sp.wait_ge(S["stored"], 32)

        @block.gpsimd
        def _(pool):
            nc.gpsimd.memset(ident[:, :], 1.0).then_inc(S["const"], 1)
            nc.gpsimd.memset(epst[:, 0:1], EPS).then_inc(S["const"], 1)
            nc.gpsimd.memset(epst[:, 1:2], TINY).then_inc(S["const"], 1)
            nc.gpsimd.memset(E[:, :, :, :], 0.0).then_inc(S["e_zero"], 1)
            pool.wait_ge(S["const"], 3)
            nc.gpsimd.affine_select(out=ident[:, :], in_=ident[:, :], compare_op=ALU.is_equal, fill=0.0, base=0,
                                    pattern=[[-1, P]], channel_multiplier=1).then_inc(S["const"], 1)
            pool.wait_ge(S["in_c"], 48)

            def scatter(i, what, src, ranked, done):
                for b in range(NB):
                    if b % 4 == 0:
                        pool.wait_ge(S[ranked], b // 4 + 1)
                    nc.gpsimd.indirect_dma_start(
                        out=what[i], out_offset=bass.IndirectOffsetOnAxis(ap=rank[:, i, b:b + 1], axis=0),
                        in_=src(b), in_offset=None).then_inc(S[done], 16)

            scatter(0, d_perm, lambda b: idt[:, b, :], "rank_r", "sc_r")
            scatter(0, d_val, lambda b: rcol[:, b:b + 1], "rank_r", "val_r")
            pool.wait_ge(S["perm_r"], 16)
            pool.wait_ge(S["xw_out"], 16)
            rows = adjT.rearrange("k (h i) -> (k h) i", h=2)

            def fetch(n):
                b, h = divmod(n, 2)
                if n >= NG:
                    pool.wait_ge(S["lo_done"], n - NG + 1)
                nc.gpsimd.indirect_dma_start(
                    out=st[n % NG], out_offset=None, in_=rows,
                    in_offset=bass.IndirectOffsetOnAxis(ap=perm[:, 0, b, h:h + 1].bitcast(U32), axis=0)).then_inc(S[f"g{n % NG}"], 16)

            for n in range(NG):
                fetch(n)
            for n in range(2 * NB):
                b, h = divmod(n, 2)
                pool.wait_ge(S["hi_done"], n + 1)
                nc.gpsimd.tensor_tensor(Alo[:, b, h * H:(h + 1) * H], st[n % NG], Ahi[:, b, h * H:(h + 1) * H],
                                        ALU.subtract).then_inc(S["lo_done"], 1)
                if n + NG < 2 * NB:
                    fetch(n + NG)
                if n == 23:
                    scatter(1, d_perm, lambda b: idt[:, b, :], "rank_c", "sc_c")
                    scatter(1, d_val, lambda b: ccol[:, b:b + 1], "rank_c", "val_c")
            pool.wait_ge(S["perm_c"], 16)
            pool.wait_ge(S["d_lo"], 2)
            pool.wait_ge(S["w_lo"], 1)
            for b in range(NB):
                nc.gpsimd.indirect_dma_start(
                    out=xws[:, b * FEAT:(b + 1) * FEAT], out_offset=None, in_=d_xw,
                    in_offset=bass.IndirectOffsetOnAxis(ap=perm[:, 1, b, 2:3].bitcast(U32), axis=0)).then_inc(S["xws_in"], 16)

            pool.wait_ge(S["cs_in"], 16)

            def pair(J0, first):
                for u in range(2):
                    for c in range(NC):
                        t = (J0 + u) * NC + c
                        if c == 0:
                            if not first:
                                pool.wait_ge(S["q_ready"], t - NC)
                            nc.gpsimd.tensor_copy(cj[:, u:u + 1], cs[:, bass.ds(J0 + u, 1)]).then_inc(S["cj_ready"], 1)
                            pool.wait_ge(S["cj_ready"], J0 + u + 1)
                        if not (first and u == 0 and c < 2):
                            pool.wait_ge(S["lz_ready"], t - 1)
                        nc.gpsimd.tensor_tensor(q_t[c % 2], rrow[:, c * W:(c + 1) * W],
                                                cj[:, u:u + 1].to_broadcast([P, W]), ALU.add).then_inc(S["q_ready"], 1)

            pair(0, True)
            with pool.Fori(1, NP2) as p:
                pair(2 * p, False)
            pool.wait_ge(S["b_out"], 16)
            for b in range(NB):
                nc.gpsimd.indirect_dma_start(
                    out=Bs[:, b * FEAT:(b + 1) * FEAT], out_offset=None, in_=d_b,
                    in_offset=bass.IndirectOffsetOnAxis(ap=perm[:, 0, b, 2:3].bitcast(U32), axis=0)).then_inc(S["b_in"], 16)

        def transpose_back(pe, c):
            pe.wait_ge(S["ht_sb"], c + 1)
            for b in range(4 * c, 4 * c + 4):
                mm = nc.tensor.transpose(num[c][:, (b % 4) * P:(b % 4 + 1) * P], HT[:, b * P:(b + 1) * P], ident[:, :])
            mm.then_inc(S["h_t"], 1)

        @block.tensor
        def _(pe):
            pe.wait_ge(S["in_w"], 32)
            nc.tensor.matmul(bt[0][:, 0:2], wTs[:, :], a2s[:, :], start=True, stop=True).then_inc(S["p_wa"], 1)
            pe.wait_ge(S["in_x"], 32)
            pe.wait_ge(S["wa_sb"], 1)
            for c in range(NC):
                mm = nc.tensor.matmul(ps[0:2, c, :], wa[:, :], xTs[:, c * W:(c + 1) * W], start=True, stop=True)
            mm.then_inc(S["p_rows"], 1)
            for b in range(NB):
                mm = nc.tensor.matmul(bt[b // 4][:, (b % 4) * P:(b % 4 + 1) * P], xTs[:, b * P:(b + 1) * P], ws[:, :],
                                      start=True, stop=True)
            mm.then_inc(S["p_xw"], 1)
            pe.wait_ge(S["rows_sb"], 1)
            pe.wait_ge(S["e_ready"], 2)
            for n in range(2 * NB):
                b, h = divmod(n, 2)
                pe.wait_ge(S["lo_done"], n + 1)
                for c in (2 * h, 2 * h + 1):
                    for i, (e, a) in enumerate(((0, Ahi), (0, Alo), (1, Ahi))):
                        mm = nc.tensor.matmul(ps[0:R, c, :], E[:, e, b, :], a[:, b, c * W:(c + 1) * W],
                                              start=(b == 0 and i == 0), stop=(b == NB - 1 and i == 2))
            mm.then_inc(S["p_sums"], 1)

            def add_bt(J, u, c, first, last):
                t = J * NC + c
                if c == 0:
                    pe.wait_ge(S["xwp_ready"], J + 1)
                pe.wait_ge(S["att_ready"], t + 1)
                nc.tensor.matmul(bt[c], xwp[:, u, :], att[c], start=first, stop=last).then_inc(S["bt_added"], 1)

            pe.wait_ge(S["sums_sb"], 1)
            pe.wait_ge(S["w_lo"], 1)
            pe.wait_ge(S["d_lo"], 2)
            pe.wait_ge(S["xw_sb"], 1)
            LAG = 3

            def pair(J0, first, last):
                for u in range(2):
                    J = J0 + u
                    lo = pe.value_load(lohi[0:1, 0, bass.ds(J, 1)], min_val=0, max_val=NB - 1)
                    hi1 = pe.value_load(lohi[0:1, 1, bass.ds(J, 1)], min_val=1, max_val=NB)
                    for c in range(NC):
                        t = J * NC + c
                        if not (first and u == 0):
                            pe.wait_ge(S["att_ready"], t - NC + 1)
                        nc.tensor.matmul(num[c], wgt[0:R, bass.ds(J * P, P)], sums[0:R, c * W:(c + 1) * W],
                                         start=True, stop=False, skip_group_check=True)
                        with pe.Fori(lo, hi1) as k:
                            slot = J + (NB - 1) - k
                            for i, (d, a) in enumerate(((0, Ahi), (0, Alo), (1, Ahi))):
                                nc.tensor.matmul(num[c], D[:, d, bass.ds(slot, 1), :], a[:, bass.ds(k, 1), c * W:(c + 1) * W],
                                                 start=False, stop=(i == 2), skip_group_check=True)
                        nc.tensor.matmul(num[c][:, 0:1], z16[:, :], z16[:, 0:1], start=False, stop=True,
                                         skip_group_check=True).then_inc(S["num_ready"], 1)
                        if not (first and u == 0 and c < LAG):
                            pu, pc = divmod(u * NC + c - LAG, NC)
                            add_bt(J0 + pu, pu % 2, pc, first and pu == 0, last and pu == 1)

            pair(0, True, False)
            with pe.Fori(1, NP2 - 1) as p:
                pair(2 * p, False, False)
            pair(NB - 2, False, True)
            for c in range(NC - LAG, NC):
                add_bt(NB - 1, 1, c, False, True)

            pe.wait_ge(S["const"], 4)
            pe.wait_ge(S["bt_sb"], 1)
            for b in range(NB):
                mm = nc.tensor.transpose(num[b // 4][:, (b % 4) * P:(b % 4 + 1) * P], BT[:, b * P:(b + 1) * P], ident[:, :])
            mm.then_inc(S["b_t"], 1)
            pe.wait_ge(S["blo_done"], 1)
            for c in range(NC):
                for k in range(NB):
                    for i, (d, a) in enumerate(((0, Ahi), (0, Alo), (1, Ahi))):
                        mm = nc.tensor.matmul(bt[c], B16[:, d, k, :], a[:, k, c * W:(c + 1) * W],
                                              start=(k == 0 and i == 0), stop=(k == NB - 1 and i == 2))
                mm.then_inc(S["ht"], 1)
                if c:
                    transpose_back(pe, c - 1)
            transpose_back(pe, NC - 1)


        @block.scalar
        def _(act):
            nc.scalar.preload_act_table_set("natural_log_exp_and_others")
            act.wait_ge(S["p_rows"], 1)
            nc.scalar.activation(srow, ps[0:2, 0:4, :].rearrange("p c w -> p (c w)"), ACT.Identity).then_inc(S["rows_sb"], 1)
            act.wait_ge(S["p_xw"], 1)
            act.wait_ge(S["rows_out"], 16)
            nc.scalar.activation(stage[:, 0:N], ps[:, 4:8, :].rearrange("p c w -> p (c w)"), ACT.Identity).then_inc(S["xw_sb"], 1)
            act.wait_ge(S["m_ready"], 1)
            nc.scalar.activation(eexp[:, 0, :], rs[:, :], ACT.Exp, bias=sc[:, 0:1]).then_inc(S["e_exp"], 1)
            nc.scalar.activation(eexp[:, 1, :], rs[:, :], ACT.Exp, bias=sc[:, 1:2], scale=SLOPE).then_inc(S["e_exp"], 1)
            for n in range(2 * NB):
                b, h = divmod(n, 2)
                act.wait_ge(S[f"g{n % NG}"], 16 * (n // NG + 1))
                nc.scalar.copy(Ahi[:, b, h * H:(h + 1) * H], st[n % NG]).then_inc(S["hi_done"], 1)
            for i, (s0, s1) in enumerate(BATCH):
                m = (s1 - s0) * P
                act.wait_ge(S["d_lz"], i + 1)
                nc.scalar.activation(tmp[:, 0:m], tmp[:, 0:m], ACT.Exp, bias=sc[:, 5:6]).then_inc(S["d_exp"], 1)
                act.wait_ge(S["d_exp"], i + 1)
                nc.scalar.copy(D[:, 0, s0:s1, :].rearrange("p s j -> p (s j)"), tmp[:, 0:m]).then_inc(S["d_hi"], 1)
            act.wait_ge(S["d_lo"], 2)
            nc.scalar.activation(tmp[0:R, :], crow[0:R, :], ACT.Exp, bias=sc[0:R, 6:7], scale=cstt[0:R, 0:1]).then_inc(S["w_exp"], 1)
            act.wait_ge(S["p_sums"], 1)
            nc.scalar.copy(sums[0:R, :], ps[0:R, 0:4, :].rearrange("p c w -> p (c w)")).then_inc(S["sums_hi"], 1)
            act.wait_ge(S["w_m"], 1)
            nc.scalar.copy(wgt[0:R, :], tmp[0:R, :]).then_inc(S["w_hi"], 1)
            act.wait_ge(S["xws_in"], 16 * NB)

            def exp_of(t, c):
                act.wait_ge(S["sub_done"], t + 1)
                nc.scalar.activation(L_t[c % 2], L_t[c % 2], ACT.Exp, bias=sc[:, 4:5]).then_inc(S["exp_done"], 1)

            def pair(J0, first):
                for u in range(2):
                    J = J0 + u
                    for c in range(NC):
                        t = J * NC + c
                        if c == 0:
                            if not first:
                                act.wait_ge(S["bt_added"], (J - 1) * NC)
                            nc.scalar.copy(xwp[:, u, :], xws[:, bass.ds(J * FEAT, FEAT)]).then_inc(S["xwp_ready"], 1)
                        act.wait_ge(S["num_ready"], t + 1)
                        if not (first and u == 0 and c < 2):
                            act.wait_ge(S["att_ready"], t - 1)
                        nc.scalar.activation(L_t[c % 2], num[c], ACT.Square, scale=1.0 / 256).then_inc(S["sq_done"], 1)
                        act.wait_ge(S["sq_done"], t + 1)
                        nc.scalar.activation(L_t[c % 2], L_t[c % 2], ACT.Ln, bias=epst[:, 1:2]).then_inc(S["ln_done"], 1)
                        if not (first and u == 0 and c == 0):
                            exp_of(t - 1, c + 1)

            pair(0, True)
            with act.Fori(1, NP2) as p:
                pair(2 * p, False)
            exp_of(NB * NC - 1, 1)

            act.wait_ge(S["bt_added"], NB * NC)
            nc.scalar.activation(BT[:, :], ps[:, 4:8, :].rearrange("p c w -> p (c w)"), ACT.Identity).then_inc(S["bt_sb"], 1)
            act.wait_ge(S["b_t"], 1)
            nc.scalar.activation(Bn[:, :], ps[:, 0:4, :].rearrange("p c w -> p (c w)"), ACT.Identity).then_inc(S["b_sb"], 1)
            act.wait_ge(S["b_in"], 16 * NB)
            nc.scalar.copy(B16[:, 0, :, :].rearrange("p b f -> p (b f)"), Bs[:, :]).then_inc(S["bhi_done"], 1)
            for c in range(NC):
                act.wait_ge(S["ht"], c + 1)
                nc.scalar.activation(HT[:, c * W:(c + 1) * W], bt[c], ACT.Identity).then_inc(S["ht_sb"], 1)
            act.wait_ge(S["var"], 1)
            nc.scalar.activation(rstd[:, :], mv[:, :, 1], ACT.Sqrt, bias=epst[:, 0:1]).then_inc(S["std"], 1)

        @block.vector
        def _(dve):
            chain = [0]

            def link(ins):
                chain[0] += 1
                ins.then_inc(S["v"], 1)
                dve.wait_ge(S["v"], chain[0])

            V = nc.vector
            dve.wait_ge(S["p_wa"], 1)
            V.tensor_copy(wa[:, :], bt[0][:, 0:2]).then_inc(S["wa_sb"], 1)
            dve.wait_ge(S["in_c"], 48)
            link(V.memset(cnt[:, :, :, :], 0.0))
            link(V.memset(z16[:, :], 0.0))

            def count_before(i, row, col, group, done):
                for b in range(4 * group, 4 * group + 4):
                    v = col[:, b:b + 1]
                    if b:
                        link(V.tensor_scalar(junk[:, 0:b * P], row[:, 0:b * P], v, None, ALU.is_ge, ALU.add,
                                             accum_out=cnt[:, i, 0, b:b + 1]))
                    link(V.tensor_scalar(junk[:, 0:N - b * P], row[:, b * P:N], v, None, ALU.is_gt, ALU.add,
                                         accum_out=cnt[:, i, 1, b:b + 1]))
                    link(V.scalar_tensor_tensor(junk[:, 0:P], row[:, b * P:(b + 1) * P], v, tri[:, :],
                                                ALU.is_equal, ALU.mult, accum_out=cnt[:, i, 2, b:b + 1]))
                g = slice(4 * group, 4 * group + 4)
                link(V.tensor_tensor(cnt[:, i, 0, g], cnt[:, i, 0, g], cnt[:, i, 1, g], ALU.add))
                V.tensor_tensor(rank[:, i, g], cnt[:, i, 0, g], cnt[:, i, 2, g], ALU.add).then_inc(S[done], 1)

            dve.wait_ge(S["row_r"], 32)
            for g in range(4):
                count_before(0, rrow, rcol, g, "rank_r")
            dve.wait_ge(S["row_c"], 32)
            count_before(1, crow, ccol, 0, "rank_c")
            dve.wait_ge(S["ends_in"], 32)
            dve.wait_ge(S["rs_in"], 16)
            link(V.tensor_scalar(sc[:, 0:1], ends[:, 0, 0:1], -1.0, None, ALU.mult))
            V.tensor_scalar(sc[:, 1:2], ends[:, 0, 0:1], -SLOPE, None, ALU.mult).then_inc(S["m_ready"], 1)
            count_before(1, crow, ccol, 1, "rank_c")
            dve.wait_ge(S["e_exp"], 2)
            dve.wait_ge(S["e_zero"], 1)
            Ef = [E[:, d, :, :].rearrange("p b r -> p (b r)") for d in range(2)]
            for d in range(2):
                for g in range(3):
                    for br in range(2):
                        o = 32 * g + NB * br
                        dst = Ef[d][:, o:o + (R + 1) * (NB - 1) + 1:R + 1]
                        if d == 0:
                            i = V.tensor_copy(dst, eexp[:, br, :])
                        else:
                            i = V.tensor_tensor(dst, eexp[:, br, :], Ef[0][:, o:o + (R + 1) * (NB - 1) + 1:R + 1], ALU.subtract)
                i.then_inc(S["e_ready"], 1)
                dve.wait_ge(S["e_ready"], d + 1)
            count_before(1, crow, ccol, 2, "rank_c")
            count_before(1, crow, ccol, 3, "rank_c")

            dve.wait_ge(S["crow_in"], 16)
            rmax, rmin = ends[:, 0, :], ends[:, 1, :]
            cmax, cmin = crow[:, 0:N:P], crow[:, P - 1:N:P]
            link(V.tensor_tensor(sc[:, 2:3], ends[:, 0, 0:1], crow[:, 0:1], ALU.add))
            link(V.scalar_tensor_tensor(sc[:, 3:4], sc[:, 2:3], SLOPE, sc[:, 2:3], ALU.mult, ALU.max))
            link(V.tensor_scalar(sc[:, 4:5], sc[:, 3:4], -1.0, None, ALU.mult))
            link(V.tensor_scalar(sc[:, 5:6], sc[:, 3:4], -1.0, DSCALE, ALU.mult, ALU.add))
            link(V.scalar_tensor_tensor(sc[:, 6:7], ends[:, 0, 0:1], cstt[:, 0:1], sc[:, 5:6], ALU.mult, ALU.add))
            jk3 = tmp[:, 0:NB * NB].rearrange("p (j k) -> p j k", j=NB)
            for o, (re, ce, op) in enumerate(((rmin, cmin, ALU.is_gt), (rmax, cmax, ALU.is_le))):
                link(V.tensor_tensor(jk3, ce.unsqueeze(2).to_broadcast([P, NB, NB]), re.unsqueeze(1).to_broadcast([P, NB, NB]), ALU.add))
                link(V.tensor_scalar(jk3, jk3, 0.0, None, op))
                link(V.tensor_reduce(t16[:, o, :], jk3, AX.X, ALU.add))
            lo, hi = t16[:, 0, :], t16[:, 1, :]
            link(V.tensor_scalar(lo, lo, float(NB - 1), None, ALU.min))
            link(V.tensor_scalar(hi, hi, -1.0, float(NB - 1), ALU.mult, ALU.add))
            link(V.tensor_tensor(hi, hi, lo, ALU.max))
            link(V.tensor_copy(lohi[:, 0, :], lo))
            link(V.tensor_scalar(lohi[:, 1, :], hi, 1.0, None, ALU.add))
            link(V.tensor_tensor(t16[:, 2, :], cstt[:, 4:4 + NB], lo, ALU.subtract))
            s3 = tmp[:, 0:NS * NB].rearrange("p (s j) -> p s j", s=NS)
            ramp = cstt[:, 4 + NB:4 + NB + NS]
            link(V.tensor_tensor(s3, t16[:, 2, :].unsqueeze(1).to_broadcast([P, NS, NB]),
                                 ramp.unsqueeze(2).to_broadcast([P, NS, NB]), ALU.is_lt))
            link(V.tensor_reduce(steps[:, 0, :], s3, AX.X, ALU.add))
            link(V.tensor_scalar(steps[:, 0, :], steps[:, 0, :], float(NB - 1), None, ALU.min))
            link(V.tensor_tensor(steps[:, 1, :], steps[:, 0, :], ramp, ALU.subtract))
            link(V.tensor_scalar(steps[:, 1, :], steps[:, 1, :], float(NB - 1), 0.0, ALU.add, ALU.max))
            link(V.tensor_scalar(steps[:, 1, :], steps[:, 1, :], float(NB - 1), None, ALU.min))
            link(V.tensor_scalar(steps[:, 0, :], steps[:, 0, :], float(P), None, ALU.mult))
            link(V.tensor_copy(jk[:, :, :], steps[:, :, :]))
            link(V.tensor_scalar(t16[:, 2, :], lo, cstt[:, 2:3], None, ALU.mult))
            link(V.scalar_tensor_tensor(t16[:, 2, :], hi, cstt[:, 3:4], t16[:, 2, :], ALU.mult, ALU.add))
            link(V.tensor_scalar(mask[:, :], t16[:, 2, :], cstt[:, 1:2], None, ALU.is_gt))
            for i, (s0, s1) in enumerate(BATCH):
                m = (s1 - s0) * P
                if i:
                    dve.wait_ge(S["d_lo"], i)
                with dve.Fori(s0, s1) as s:
                    jc = dve.value_load(jk[0:1, 0, bass.ds(s, 1)], min_val=0, max_val=(NB - 1) * P)
                    kb = dve.value_load(jk[0:1, 1, bass.ds(s, 1)], min_val=0, max_val=NB - 1)
                    V.tensor_scalar(tmp[:, bass.ds((s - s0) * P, P)], crow[:, bass.ds(jc, P)], rs[:, bass.ds(kb, 1)], None,
                                    ALU.add).then_inc(S["d_z"], 1)
                dve.wait_ge(S["d_z"], s1)
                V.scalar_tensor_tensor(tmp[:, 0:m], tmp[:, 0:m], SLOPE, tmp[:, 0:m], ALU.mult, ALU.max).then_inc(S["d_lz"], 1)
                dve.wait_ge(S["d_hi"], i + 1)
                V.tensor_tensor(D[:, 1, s0:s1, :].rearrange("p s j -> p (s j)"), tmp[:, 0:m],
                                D[:, 0, s0:s1, :].rearrange("p s j -> p (s j)"), ALU.subtract).then_inc(S["d_lo"], 1)
            dve.wait_ge(S["w_exp"], 1)
            w3 = tmp[0:R, :].rearrange("p (b j) -> p b j", b=NB)
            V.tensor_tensor(w3, w3, mask[0:R, :].unsqueeze(2).to_broadcast([R, NB, P]), ALU.mult).then_inc(S["w_m"], 1)
            dve.wait_ge(S["w_hi"], 1)
            V.tensor_tensor(wgt[64:R, :], tmp[64:R, :], wgt[64:R, :], ALU.subtract).then_inc(S["w_lo"], 1)
            dve.wait_ge(S["sums_hi"], 1)
            V.tensor_tensor(sums[32:64, :], ps[32:64, 0:4, :].rearrange("p c w -> p (c w)"), sums[32:64, :],
                            ALU.subtract).then_inc(S["sums_sb"], 1)

            def att_of(t, c, first):
                dve.wait_ge(S["exp_done"], t + 1)
                if not first:
                    dve.wait_ge(S["bt_added"], t - NC + 1)
                V.scalar_tensor_tensor(att[c], num[c], 1.0 / 256, L_t[c % 2], ALU.mult, ALU.mult).then_inc(S["att_ready"], 1)

            def pair(J0, first):
                for u in range(2):
                    J = J0 + u
                    for c in range(NC):
                        t = J * NC + c
                        dve.wait_ge(S["q_ready"], t + 1)
                        if not (first and u == 0 and c < 2):
                            dve.wait_ge(S["sub_done"], t - 1)
                        V.scalar_tensor_tensor(lz_t[c % 2], q_t[c % 2], SLOPE, q_t[c % 2], ALU.mult, ALU.max).then_inc(S["lz_ready"], 1)
                        dve.wait_ge(S["lz_ready"], t + 1)
                        dve.wait_ge(S["ln_done"], t + 1)
                        V.tensor_tensor(L_t[c % 2], lz_t[c % 2], L_t[c % 2], ALU.subtract).then_inc(S["sub_done"], 1)
                        if not (first and u == 0 and c == 0):
                            att_of(t - 1, (c - 1) % NC, first and (u == 0 or c == 0))

            pair(0, True)
            with dve.Fori(1, NP2) as p:
                pair(2 * p, False)
            att_of(NB * NC - 1, NC - 1, False)

            dve.wait_ge(S["bhi_done"], 1)
            V.tensor_tensor(B16[:, 1, :, :].rearrange("p b f -> p (b f)"), Bs[:, :],
                            B16[:, 0, :, :].rearrange("p b f -> p (b f)"), ALU.subtract).then_inc(S["blo_done"], 1)
            dve.wait_ge(S["x_in"], 16)
            dve.wait_ge(S["b_out"], 16)
            for c in range(NC):
                dve.wait_ge(S["h_t"], c + 1)
                for b in range(4 * c, 4 * c + 4):
                    link(V.tensor_tensor(y[:, b, :], xs[:, b * FEAT:(b + 1) * FEAT], num[c][:, (b % 4) * P:(b % 4 + 1) * P], ALU.add))
                    link(V.bn_stats(stats[:, b, :], y[:, b, :]))
                    i = V.bn_aggr(mv[:, b, :], stats[:, b, :])
            i.then_inc(S["var"], 1)
            dve.wait_ge(S["std"], 1)
            link(V.reciprocal(rstd[:, :], rstd[:, :]))
            for b in range(NB):
                i = V.tensor_scalar(y[:, b, :], y[:, b, :], mv[:, b, 0:1], rstd[:, b:b + 1], ALU.subtract, ALU.mult)
                if b % 8 == 7:
                    i.then_inc(S["y_ready"], 1)


def kernel(x, adj, L0_gnn_W, L0_gnn_a):
    import concourse.bacc as bacc
    from concourse.bass_utils import run_bass_kernel_spmd

    x, w, a = np.asarray(x), np.asarray(L0_gnn_W), np.asarray(L0_gnn_a)
    cst, before, ids = constants()
    arrays = {
        "xT": np.ascontiguousarray(x.T),
        "x": np.ascontiguousarray(x),
        "adjT": np.ascontiguousarray(np.asarray(adj).T),
        "w": np.ascontiguousarray(w),
        "wT": np.ascontiguousarray(w.T),
        "a2": np.ascontiguousarray(a.reshape(2, FEAT).T),
        "cst": np.ascontiguousarray(cst),
        "before": before,
        "ids": np.ascontiguousarray(ids),
    }
    nc = bacc.Bacc("TRN2", target_bir_lowering=False, num_devices=1)
    args = [nc.dram_tensor(n, v.shape, mybir.dt.from_np(v.dtype), kind="ExternalInput").ap() for n, v in arrays.items()]
    args.append(nc.dram_tensor("out", x.shape, mybir.dt.float32, kind="ExternalOutput").ap())
    graph_attention_layernorm(nc, *args)
    r = run_bass_kernel_spmd(nc, [arrays], core_ids=[0])
    return r.results[0]["out"]
```

```python
import concourse.bass as bass
from concourse import mybir
from contextlib import ExitStack
import numpy as np

P = 128
W = 512
FEAT = 128
SLOPE = 0.01
EPS = 1e-5
TINY = 1e-18
NODES = 2048
NB = NODES // P
NS = 2 * NB - 1
BATCH = tuple((s, min(s + NB // 2, NS)) for s in range(0, NS, NB // 2))
STAIR = NB + 4
LOS = 4
R = 96
DSCALE = 8 * float(np.log(2.0))


def constants():
    q = np.arange(P)
    b = (q % 32) // NB
    cols = [np.where(b == 0, 1.0, SLOPE), np.where(b == 0, q % NB, -(q % NB)), 1.0 - b, -1.0 * b]
    rows = np.concatenate([np.arange(NB) + NB - 1.0, np.arange(NS) * 1.0])
    cst = np.concatenate([np.stack(cols, 1), np.broadcast_to(rows, (P, rows.size))], 1).astype(np.float32)
    before = (q[:, None] < q[None, :]).astype(np.float32)
    ids = np.stack(np.broadcast_arrays(np.arange(NB)[None, :], q[:, None]), 2).astype(np.float32)
    return cst, before, ids


def graph_attention_layernorm(nc, xT, x, adjT, w, wT, a2, cst, before, ids, out):
    F32 = mybir.dt.float32
    F16 = mybir.dt.float16
    BF16 = mybir.dt.bfloat16
    I32 = mybir.dt.int32
    U32 = mybir.dt.uint32
    ALU = mybir.AluOpType
    ACT = mybir.ActivationFunctionType
    AX = mybir.AxisListType
    N = NODES
    NC = N // W
    NP2 = NB // 2
    H = N // 2
    NG = 3

    ctx = ExitStack()
    with ctx:
        def sb(name, shape, dt=F32):
            return ctx.enter_context(nc.sbuf_tensor(name, shape, dt))

        def sem(name):
            return ctx.enter_context(nc.semaphore(name))

        def dram(name, shape, dt=F32):
            return nc.dram_tensor(name, shape, dt, kind="Internal").ap()

        Ahi = sb("Ahi", [P, NB, N], F16)
        Alo = sb("Alo", [P, NB, N], F16)
        stage = sb("stage", [P, NG * H])
        rrow = sb("rrow", [P, N])
        crow = sb("crow", [P, N])
        D = sb("D", [P, 2, NS, P], F16)
        xws = sb("xws", [P, N])
        tmp = sb("tmp", [P, N])
        wgt = sb("wgt", [P, N], F16)
        sums = sb("sums", [P, N], F16)
        E = sb("E", [P, 2, NB, R], F16)
        rcol = sb("rcol", [P, NB])
        ccol = sb("ccol", [P, NB])
        rs = sb("rs", [P, NB])
        cs = sb("cs", [P, NB])
        rank = sb("rank", [P, 2, NB])
        ranku = sb("ranku", [P, NB], U32)
        rest = sb("rest", [P, NB])
        perm = sb("perm", [P, 2, 3, NB], U32)
        onesb = sb("onesb", [P, 1], BF16)
        rslot = sb("rslot", [P, NS])
        cstt = sb("cstt", [P, 4 + NB + NS])
        ident = sb("ident", [P, P])
        a2s = sb("a2s", [P, 2])
        xwp = sb("xwp", [P, 2, FEAT])
        ends = sb("ends", [P, 2, NB])
        sc = sb("sc", [P, 8])
        t16 = sb("t16", [P, 4, NB])
        eexp = sb("eexp", [P, 2, NB])
        steps = sb("steps", [P, 2, NS])
        lohi = sb("lohi", [P, 2, NB], I32)
        jk = sb("jk", [P, NS], I32)
        mask = sb("mask", [P, NB])
        epst = sb("epst", [P, 2])
        stats = sb("stats", [P, NB, 6])
        mv = sb("mv", [P, NB, 2])
        rstd = sb("rstd", [P, NB])
        cj = sb("cj", [P, 2])
        z16 = sb("z16", [P, P], F16)

        xTs = tmp
        wTs = stage[:, N:N + FEAT]
        ws = stage[:, N + FEAT:N + 2 * FEAT]
        wa = stage[:, N + 2 * FEAT:N + 4 * FEAT].rearrange("p (i q) -> p i q", i=2)
        vals = xws[:, 0:5 * NB].bitcast(BF16).rearrange("p (i b v) -> p i b v", i=2, v=5)
        sorted5 = xws[:, 128:128 + 10 * NB].rearrange("p (i b v) -> p i b v", i=2, v=5)
        tie = xws[:, 384:384 + 3 * P // 2].bitcast(BF16).rearrange("p (i q) -> p i q", i=3)
        tri = xws[:, 640:640 + P]
        idt = xws[:, 768:768 + 2 * NB].rearrange("p (b v) -> p b v", v=2)
        flags = [D[:, :, :, :].rearrange("p a s j -> p (a s j)")[:, i * N:(i + 1) * N].bitcast(BF16) for i in range(3)]
        ramp16 = wgt
        st = [stage[:, g * H:(g + 1) * H] for g in range(NG)]
        q_t = [crow[:, 0:W], crow[:, W:2 * W]]
        lz_t = [crow[:, 2 * W:3 * W], crow[:, 3 * W:4 * W]]
        L_t = [tmp[:, i * W:(i + 1) * W] for i in range(NC)]
        att = [stage[:, (2 + i) * W:(3 + i) * W] for i in range(4)]
        BT = rrow
        Bn = crow
        Bs = xws
        B16 = D[:, :, 0:NB, :]
        HT = rrow
        xs = stage[:, 0:N]
        y = crow[:, :].rearrange("p (b f) -> p b f", b=NB)

        d_xw = dram("d_xw", [N, FEAT])
        d_rs = dram("d_rs", [P, NB])
        d_b = dram("d_b", [N, FEAT])

        ps = ctx.enter_context(nc.psum_tensor("ps", [P, 8, W], F32))
        num = [ps[:, c, :] for c in range(NC)]
        bt = [ps[:, NC + c, :] for c in range(NC)]

        names = """in_w in_x in_c p_wa wa_sb p_row p_col r_even r_odd row_c rcol_sb ccol_sb p_xw xw_sb xw_out
            const ramp flags flags_used ranked_sb placed perm_r perm_c rs_out ends_in crow_t crow_sb
            slots_ready mask_ready g0 g1 g2 hi_done lo_dve lo_pool e_zero e_ready p_sums sums_hi sums_sb
            m_ready e_exp v d_z d_lz d_exp d_lo w_exp w_m w_hi w_lo xws_in cj_ready num_ready q_ready
            lz_ready sq_done ln_done sub_done exp_done att_ready bt_added xwp_ready bt_sb b_t b_sb b_out
            b_in0 b_in1 bhi_done blo_done ht ht_sb h_t x_in var std y_ready stored""".split()
        S = {n: sem(n) for n in names}
        block = ctx.enter_context(nc.Block())

        def wait_lo(engine, n):
            engine.wait_ge(S["lo_dve"], n + 1 - (n + 1) // LOS)
            if n + 1 >= LOS:
                engine.wait_ge(S["lo_pool"], (n + 1) // LOS)

        def batch(i):
            s0, s1 = BATCH[i]
            o = (i % 2) * (N // 2)
            return (tmp[:, o:o + (s1 - s0) * P], [D[:, d, s0:s1, :].rearrange("p s j -> p (s j)") for d in range(2)], s1)

        def c_steps(n):
            if n < NB // 2:
                return range(2 * n, 2 * n + 2)
            n -= 1
            return range(2 * n, 2 * n + 2) if NB // 2 <= n < NB else range(0)

        @block.sync
        def _(sp):
            sp.dma_start(wTs[:, :], wT).then_inc(S["in_w"], 16)
            sp.dma_start(a2s[:, :], a2).then_inc(S["in_w"], 16)
            sp.dma_start(xTs[:, :], xT).then_inc(S["in_x"], 16)
            sp.dma_start(ws[:, :], w).then_inc(S["in_x"], 16)
            sp.dma_start(tri[:, :], before).then_inc(S["in_c"], 16)
            sp.dma_start(idt[:, :, :], ids).then_inc(S["in_c"], 16)
            sp.dma_start(cstt[:, :], cst).then_inc(S["in_c"], 16)
            sp.wait_ge(S["xw_sb"], 1)
            sp.dma_start(d_xw.rearrange("(b p) f -> p b f", p=P), stage[:, 0:N].rearrange("p (b f) -> p b f", b=NB)
                         ).then_inc(S["xw_out"], 16)
            sp.wait_ge(S["perm_r"], 1)
            sp.dma_start(d_rs, rs[:, :]).then_inc(S["rs_out"], 16)
            sp.wait_ge(S["rs_out"], 16)
            sp.dma_start(ends[:, 0, :], d_rs[0:1, :].to_broadcast([P, NB])).then_inc(S["ends_in"], 16)
            sp.dma_start(ends[:, 1, :], d_rs[P - 1:P, :].to_broadcast([P, NB])).then_inc(S["ends_in"], 16)
            sp.wait_ge(S["bt_added"], NB * NC)
            sp.dma_start(xs.rearrange("p (b f) -> p b f", b=NB), x.rearrange("(b p) f -> p b f", p=P)).then_inc(S["x_in"], 16)
            sp.wait_ge(S["b_out"], 16 * NB)
            for g in range(2):
                sp.dma_start(Bs[:, g * N // 2:(g + 1) * N // 2].rearrange("p (b f) -> p b f", b=NB // 2),
                             d_b.rearrange("(b p) f -> p b f", p=P)[:, g * NB // 2:(g + 1) * NB // 2, :]).then_inc(S[f"b_in{g}"], 16)
            for c in range(NC):
                sp.wait_ge(S["y_ready"], c + 1)
                sp.dma_start(out.rearrange("(b p) f -> p b f", p=P)[:, 4 * c:4 * c + 4, :],
                             y[:, 4 * c:4 * c + 4, :]).then_inc(S["stored"], 16)
            sp.wait_ge(S["stored"], 16 * NC)

        @block.gpsimd
        def _(pool):
            nc.gpsimd.memset(ident[:, :], 1.0).then_inc(S["const"], 1)
            nc.gpsimd.memset(epst[:, 0:1], EPS).then_inc(S["const"], 1)
            nc.gpsimd.memset(epst[:, 1:2], TINY).then_inc(S["const"], 1)
            nc.gpsimd.memset(E[:, :, :, :], 0.0).then_inc(S["e_zero"], 1)
            pool.wait_ge(S["const"], 3)
            nc.gpsimd.affine_select(out=ident[:, :], in_=ident[:, :], compare_op=ALU.is_equal, fill=0.0, base=0,
                                    pattern=[[-1, P]], channel_multiplier=1).then_inc(S["const"], 1)

            nc.gpsimd.iota(ramp16[:, :], pattern=[[1, N]], base=0, channel_multiplier=0,
                           allow_small_or_imprecise_dtypes=True).then_inc(S["ramp"], 1)
            nc.gpsimd.memset(onesb[:, :], 1.0).then_inc(S["const"], 1)
            pool.wait_ge(S["perm_r"], 1)
            pool.wait_ge(S["xw_out"], 16)
            rows = adjT.rearrange("k (h i) -> (k h) i", h=2)

            def fetch(n):
                b, h = divmod(n, 2)
                if n >= NG:
                    wait_lo(pool, n - NG)
                nc.gpsimd.indirect_dma_start(
                    out=st[n % NG], out_offset=None, in_=rows,
                    in_offset=bass.IndirectOffsetOnAxis(ap=perm[:, 0, h, b:b + 1], axis=0)).then_inc(S[f"g{n % NG}"], 16)

            for n in range(NG):
                fetch(n)
            for n in range(2 * NB):
                b, h = divmod(n, 2)
                if n % LOS == LOS - 1:
                    pool.wait_ge(S["hi_done"], n + 1)
                    nc.gpsimd.tensor_tensor(Alo[:, b, h * H:(h + 1) * H], st[n % NG], Ahi[:, b, h * H:(h + 1) * H],
                                            ALU.subtract).then_inc(S["lo_pool"], 1)
                if n + NG < 2 * NB:
                    fetch(n + NG)
                if n == STAIR + 1:
                    pool.wait_ge(S["mask_ready"], 1)
                    pool.wait_ge(S["w_exp"], 1)
                    w3 = tmp[0:R, :].rearrange("p (b j) -> p b j", b=NB)
                    nc.gpsimd.tensor_tensor(w3, w3, mask[0:R, :].unsqueeze(2).to_broadcast([R, NB, P]), ALU.mult
                                            ).then_inc(S["w_m"], 1)
                if n == NB + 2:
                    pool.wait_ge(S["perm_c"], 1)
                if NB + 2 <= n < NB + 2 + NB // 2:
                    for b in range(2 * (n - NB - 2), 2 * (n - NB - 1)):
                        nc.gpsimd.indirect_dma_start(
                            out=xws[:, b * FEAT:(b + 1) * FEAT], out_offset=None, in_=d_xw,
                            in_offset=bass.IndirectOffsetOnAxis(ap=perm[:, 1, 2, b:b + 1], axis=0)).then_inc(S["xws_in"], 16)

            pool.wait_ge(S["d_z"], NS)

            def pair(J0, first):
                for u in range(2):
                    for c in range(NC):
                        t = (J0 + u) * NC + c
                        if c == 0:
                            if not first:
                                pool.wait_ge(S["q_ready"], t - NC)
                            nc.gpsimd.tensor_copy(cj[:, u:u + 1], cs[:, bass.ds(J0 + u, 1)]).then_inc(S["cj_ready"], 1)
                            pool.wait_ge(S["cj_ready"], J0 + u + 1)
                        if not (first and u == 0 and c < 2):
                            pool.wait_ge(S["lz_ready"], t - 1)
                        nc.gpsimd.tensor_tensor(q_t[c % 2], rrow[:, c * W:(c + 1) * W],
                                                cj[:, u:u + 1].to_broadcast([P, W]), ALU.add).then_inc(S["q_ready"], 1)

            pair(0, True)
            with pool.Fori(1, NP2) as p:
                pair(2 * p, False)
            for b in range(NB):
                if b % 4 == 0:
                    pool.wait_ge(S["b_sb"], b // 4 + 1)
                nc.gpsimd.indirect_dma_start(
                    out=d_b, out_offset=bass.IndirectOffsetOnAxis(ap=ranku[:, b:b + 1], axis=0),
                    in_=Bn[:, b * FEAT:(b + 1) * FEAT], in_offset=None).then_inc(S["b_out"], 16)

        def transpose_back(pe, c):
            pe.wait_ge(S["ht_sb"], c + 1)
            for b in range(4 * c, 4 * c + 4):
                mm = nc.tensor.transpose(num[c][:, (b % 4) * P:(b % 4 + 1) * P], HT[:, b * P:(b + 1) * P], ident[:, :])
            mm.then_inc(S["h_t"], 1)

        @block.tensor
        def _(pe):
            pe.wait_ge(S["in_w"], 32)
            nc.tensor.matmul(bt[0][:, 0:2], wTs[:, :], a2s[:, :], start=True, stop=True).then_inc(S["p_wa"], 1)
            pe.wait_ge(S["in_x"], 32)
            pe.wait_ge(S["wa_sb"], 1)
            pe.wait_ge(S["const"], 4)
            for i in (1, 0):
                if i == 0:
                    pe.wait_ge(S["r_even"], 2)
                    pe.wait_ge(S["r_odd"], 2)
                for c in range(NC):
                    nc.tensor.matmul(num[c], wa[:, i, :], xTs[:, c * W:(c + 1) * W], start=True, stop=True).then_inc(S["p_row"], 1)
                if i == 0:
                    pe.wait_ge(S["row_c"], 1)
                for b in range(NB):
                    if i and b % 4 == 0:
                        h, c = divmod(b // 4, 2)
                        pe.wait_ge(S["r_odd"] if c else S["r_even"], h + 1)
                    mm = nc.tensor.transpose(bt[2 + i][:, 32 * b:32 * b + 32], (rrow if i else crow)[0:32, b * P:(b + 1) * P],
                                             ident[0:32, 0:32])
                mm.then_inc(S["p_col"], 1)
            for b in range(NB):
                mm = nc.tensor.matmul(num[b // 4][:, (b % 4) * P:(b % 4 + 1) * P], xTs[:, b * P:(b + 1) * P], ws[:, :],
                                      start=True, stop=True)
            mm.then_inc(S["p_xw"], 1)

            def sort_step(i, step):
                f = i * 2 * NB + step
                fl = flags[f % 3]
                b = step % NB
                if i and b == 0:
                    pe.wait_ge(S["ranked_sb"] if step < NB else S["placed"], 1)
                pe.wait_ge(S["flags"], f + 1)
                for kb in range(NB):
                    if step < NB:
                        mm = nc.tensor.matmul(bt[0][:, kb:kb + 1], fl[:, kb * P:(kb + 1) * P], onesb[:, :],
                                              start=(b == 0 and kb == 0), stop=(b == NB - 1), skip_group_check=True)
                    else:
                        mm = nc.tensor.matmul(bt[1][:, 5 * kb:5 * kb + 5], fl[:, kb * P:(kb + 1) * P], vals[:, i, b, :],
                                              start=(b == 0 and kb == 0), stop=(b == NB - 1), skip_group_check=True)
                if step < NB:
                    mm = nc.tensor.matmul(bt[0][:, b:b + 1], tie[:, f % 3, :], onesb[:, :], start=False, stop=(b == NB - 1),
                                          skip_group_check=True)
                mm.then_inc(S["flags_used"], 1)

            pe.wait_ge(S["const"], 5)
            for step in range(2 * NB):
                sort_step(0, step)
            pe.wait_ge(S["xw_sb"], 1)
            for n in range(2 * NB):
                for step in c_steps(n):
                    sort_step(1, step)
                if n == NB + 2:
                    pe.wait_ge(S["perm_c"], 1)
                    for b in range(NB):
                        mm = nc.tensor.matmul(bt[b // 4][:, (b % 4) * P:(b % 4 + 1) * P], cs[:, b:b + 1].to_broadcast([P, P]),
                                              ident[:, :], start=True, stop=True)
                    mm.then_inc(S["crow_t"], 1)
                if n == 0:
                    pe.wait_ge(S["e_ready"], 2)
                b, h = divmod(n, 2)
                wait_lo(pe, n)
                for c in (2 * h, 2 * h + 1):
                    for i, (e, a) in enumerate(((0, Ahi), (0, Alo), (1, Ahi))):
                        mm = nc.tensor.matmul(ps[0:R, c, :], E[:, e, b, :], a[:, b, c * W:(c + 1) * W],
                                              start=(b == 0 and i == 0), stop=(b == NB - 1 and i == 2))
                if b == NB - 1:
                    mm.then_inc(S["p_sums"], 1)

            def add_bt(J, u, c, first, last):
                t = J * NC + c
                if c == 0:
                    pe.wait_ge(S["xwp_ready"], J + 1)
                pe.wait_ge(S["att_ready"], t + 1)
                nc.tensor.matmul(bt[c], xwp[:, u, :], att[c], start=first, stop=last).then_inc(S["bt_added"], 1)

            pe.wait_ge(S["w_lo"], 1)
            pe.wait_ge(S["d_lo"], len(BATCH))
            LAG = 3

            def ends_of(J):
                return (pe.value_load(lohi[0:1, 0, bass.ds(J, 1)], min_val=0, max_val=NB - 1),
                        pe.value_load(lohi[0:1, 1, bass.ds(J, 1)], min_val=1, max_val=NB))

            def pair(J0, first, last):
                for u in range(2):
                    J = J0 + u
                    if u == 0:
                        lo, hi1 = ends_of(J)
                    else:
                        lo, hi1 = lo_next, hi1_next
                    for c in range(NC):
                        if u == 0 and c == NC - 1:
                            lo_next, hi1_next = ends_of(J + 1)
                        t = J * NC + c
                        if first and u == 0:
                            pe.wait_ge(S["sums_sb"], c + 1)
                        else:
                            pe.wait_ge(S["att_ready"], t - NC + 1)
                        nc.tensor.matmul(num[c], wgt[0:R, bass.ds(J * P, P)], sums[0:R, c * W:(c + 1) * W],
                                         start=True, stop=False, skip_group_check=True)
                        with pe.Fori(lo, hi1) as k:
                            slot = J + (NB - 1) - k
                            for i, (d, a) in enumerate(((0, Ahi), (0, Alo), (1, Ahi))):
                                nc.tensor.matmul(num[c], D[:, d, bass.ds(slot, 1), :], a[:, bass.ds(k, 1), c * W:(c + 1) * W],
                                                 start=False, stop=(i == 2), skip_group_check=True)
                        nc.tensor.matmul(num[c][:, 0:1], z16[:, :], z16[:, 0:1], start=False, stop=True,
                                         skip_group_check=True).then_inc(S["num_ready"], 1)
                        if not (first and u == 0 and c < LAG):
                            pu, pc = divmod(u * NC + c - LAG, NC)
                            add_bt(J0 + pu, pu % 2, pc, first and pu == 0, last and pu == 1)

            pair(0, True, False)
            with pe.Fori(1, NP2 - 1) as p:
                pair(2 * p, False, False)
            pair(NB - 2, False, True)

            def transpose_b(c):
                pe.wait_ge(S["bt_sb"], c + 1)
                for b in range(4 * c, 4 * c + 4):
                    mm = nc.tensor.transpose(num[c][:, (b % 4) * P:(b % 4 + 1) * P], BT[:, b * P:(b + 1) * P], ident[:, :])
                mm.then_inc(S["b_t"], 1)

            for c in range(NC - LAG, NC):
                add_bt(NB - 1, 1, c, False, True)
                transpose_b(c - 1)
            transpose_b(NC - 1)
            for c in range(NC):
                for k in range(NB):
                    if c == 0 and k % (NB // 2) == 0:
                        pe.wait_ge(S["blo_done"], k // (NB // 2) + 1)
                    for i, (d, a) in enumerate(((0, Ahi), (0, Alo), (1, Ahi))):
                        mm = nc.tensor.matmul(bt[c], B16[:, d, k, :], a[:, k, c * W:(c + 1) * W],
                                              start=(k == 0 and i == 0), stop=(k == NB - 1 and i == 2))
                mm.then_inc(S["ht"], 1)
                if c:
                    transpose_back(pe, c - 1)
            transpose_back(pe, NC - 1)

        @block.scalar
        def _(act):
            nc.scalar.preload_act_table_set("natural_log_exp_and_others")
            for c in (0, 2):
                act.wait_ge(S["p_row"], c + 1)
                nc.scalar.copy(rrow[:, c * W:(c + 1) * W], num[c]).then_inc(S["r_even"], 1)
            act.wait_ge(S["p_row"], 2 * NC)
            nc.scalar.copy(crow[:, :], ps[:, 0:4, :].rearrange("p c w -> p (c w)")).then_inc(S["row_c"], 1)
            act.wait_ge(S["p_xw"], 1)
            nc.scalar.copy(stage[:, 0:N], ps[:, 0:4, :].rearrange("p c w -> p (c w)")).then_inc(S["xw_sb"], 1)
            act.wait_ge(S["m_ready"], 1)
            nc.scalar.activation(eexp[:, 0, :], rs[:, :], ACT.Exp, bias=sc[:, 0:1]).then_inc(S["e_exp"], 1)
            nc.scalar.activation(eexp[:, 1, :], rs[:, :], ACT.Exp, bias=sc[:, 1:2], scale=SLOPE).then_inc(S["e_exp"], 1)
            for n in range(2 * NB):
                b, h = divmod(n, 2)
                act.wait_ge(S[f"g{n % NG}"], 16 * (n // NG + 1))
                nc.scalar.copy(Ahi[:, b, h * H:(h + 1) * H], st[n % NG]).then_inc(S["hi_done"], 1)
                if n == NB + 2:
                    act.wait_ge(S["crow_t"], 1)
                    nc.scalar.copy(crow[:, :], ps[:, 4:8, :].rearrange("p c w -> p (c w)")).then_inc(S["crow_sb"], 1)
                if n == STAIR + 1:
                    act.wait_ge(S["slots_ready"], 1)
                    nc.scalar.activation(tmp[0:R, :], crow[0:R, :], ACT.Exp, bias=sc[0:R, 6:7], scale=cstt[0:R, 0:1]
                                         ).then_inc(S["w_exp"], 1)
                    jc = nc.values_load_multi_w_load_instructions(
                        jk[0:1, :], engines=[mybir.EngineType.Activation], min_val=0, max_val=(NB - 1) * P,
                        skip_runtime_bounds_check_because="a multiple of 128 below N")[1]
                if n == STAIR + 2:
                    act.wait_ge(S["w_m"], 1)
                    nc.scalar.copy(wgt[0:R, :], tmp[0:R, :]).then_inc(S["w_hi"], 1)
                for i in range(len(BATCH)):
                    z, _, s1 = batch(i)
                    if n == STAIR + 3 + 2 * i:
                        if i == 0:
                            act.wait_ge(S["w_lo"], 1)
                        if i >= 2:
                            act.wait_ge(S["d_lo"], i - 1)
                        for s in range(BATCH[i][0], s1):
                            o = (s - BATCH[i][0]) * P
                            nc.scalar.activation(z[:, o:o + P], crow[:, bass.ds(jc[s], P)], ACT.Identity, bias=rslot[:, s:s + 1]
                                                 ).then_inc(S["d_z"], 1)
                    if n == STAIR + 4 + 2 * i:
                        act.wait_ge(S["d_lz"], i + 1)
                        nc.scalar.activation(z, z, ACT.Exp, bias=sc[:, 5:6]).then_inc(S["d_exp"], 1)
            for c in range(NC):
                act.wait_ge(S["p_sums"], c // 2 + 1)
                nc.scalar.copy(sums[0:R, c * W:(c + 1) * W], ps[0:R, c, :]).then_inc(S["sums_hi"], 1)
            act.wait_ge(S["xws_in"], 16 * NB)
            act.wait_ge(S["d_lo"], len(BATCH))

            def exp_of(t, c):
                act.wait_ge(S["sub_done"], t + 1)
                nc.scalar.activation(L_t[c], L_t[c], ACT.Exp, bias=sc[:, 4:5]).then_inc(S["exp_done"], 1)

            def pair(J0, first):
                for u in range(2):
                    J = J0 + u
                    for c in range(NC):
                        t = J * NC + c
                        if c == 0:
                            if not first:
                                act.wait_ge(S["bt_added"], (J - 1) * NC)
                            nc.scalar.copy(xwp[:, u, :], xws[:, bass.ds(J * FEAT, FEAT)]).then_inc(S["xwp_ready"], 1)
                        act.wait_ge(S["num_ready"], t + 1)
                        if not (first and u == 0):
                            act.wait_ge(S["att_ready"], t - NC + 1)
                        nc.scalar.activation(L_t[c], num[c], ACT.Square, scale=1.0 / 256).then_inc(S["sq_done"], 1)
                        act.wait_ge(S["sq_done"], t + 1)
                        nc.scalar.activation(L_t[c], L_t[c], ACT.Ln, bias=epst[:, 1:2]).then_inc(S["ln_done"], 1)
                        if not (first and u == 0 and c == 0):
                            exp_of(t - 1, (c - 1) % NC)

            pair(0, True)
            with act.Fori(1, NP2) as p:
                pair(2 * p, False)
            exp_of(NB * NC - 1, NC - 1)

            def b_out(c):
                act.wait_ge(S["b_t"], c + 1)
                nc.scalar.activation(Bn[:, c * W:(c + 1) * W], num[c], ACT.Identity).then_inc(S["b_sb"], 1)

            for c in range(NC):
                act.wait_ge(S["bt_added"], (NB - 1) * NC + c + 1)
                nc.scalar.activation(BT[:, c * W:(c + 1) * W], bt[c], ACT.Identity).then_inc(S["bt_sb"], 1)
                if c:
                    b_out(c - 1)
            b_out(NC - 1)
            for g in range(2):
                act.wait_ge(S[f"b_in{g}"], 16)
                nc.scalar.copy(B16[:, 0, g * NB // 2:(g + 1) * NB // 2, :].rearrange("p b f -> p (b f)"),
                               Bs[:, g * N // 2:(g + 1) * N // 2]).then_inc(S["bhi_done"], 1)
            for c in range(NC):
                act.wait_ge(S["ht"], c + 1)
                nc.scalar.copy(HT[:, c * W:(c + 1) * W], bt[c]).then_inc(S["ht_sb"], 1)
            for c in range(NC):
                act.wait_ge(S["var"], c + 1)
                nc.scalar.activation(rstd[:, 4 * c:4 * c + 4], mv[:, 4 * c:4 * c + 4, 1], ACT.Sqrt, bias=epst[:, 0:1]
                                     ).then_inc(S["std"], 1)

        @block.vector
        def _(dve):
            chain = [0]

            def link(ins):
                chain[0] += 1
                ins.then_inc(S["v"], 1)
                dve.wait_ge(S["v"], chain[0])

            V = nc.vector
            dve.wait_ge(S["p_wa"], 1)
            V.tensor_copy(wa[:, :, :], bt[0][:, 0:2].unsqueeze(2).to_broadcast([P, 2, P])).then_inc(S["wa_sb"], 1)
            for c in (1, 3):
                dve.wait_ge(S["p_row"], c + 1)
                V.tensor_copy(rrow[:, c * W:(c + 1) * W], num[c]).then_inc(S["r_odd"], 1)
            dve.wait_ge(S["in_c"], 48)
            link(V.memset(z16[:, :], 0.0))

            def values(i, col):
                link(V.tensor_copy(vals[:, i, :, 0:2], idt[:, :, :]))
                link(V.tensor_copy(vals[:, i, :, 2], col[:, :]))
                link(V.tensor_tensor(rest[:, :], col[:, :], vals[:, i, :, 2], ALU.subtract))
                link(V.tensor_copy(vals[:, i, :, 3], rest[:, :]))
                link(V.tensor_tensor(rest[:, :], rest[:, :], vals[:, i, :, 3], ALU.subtract))
                link(V.tensor_copy(vals[:, i, :, 4], rest[:, :]))

            def sort_step(i, row, col, step):
                f = i * 2 * NB + step
                fl = flags[f % 3]
                b = step % NB
                if f >= 3:
                    dve.wait_ge(S["flags_used"], f - 2)
                if step < NB:
                    v = col[:, b:b + 1]
                    m = (b + 1) * P
                    V.tensor_scalar(fl[:, 0:m], row[:, 0:m], v, None, ALU.is_lt)
                    if m < N:
                        V.tensor_scalar(fl[:, m:N], row[:, m:N], v, None, ALU.is_le)
                    V.scalar_tensor_tensor(tie[:, f % 3, :], row[:, b * P:m], v, tri[:, :], ALU.is_equal, ALU.mult
                                           ).then_inc(S["flags"], 1)
                else:
                    V.tensor_scalar(fl[:, :], ramp16[:, :], rank[:, i, b:b + 1], None, ALU.is_equal).then_inc(S["flags"], 1)

            def fetch_ranks(i):
                dve.wait_ge(S["flags_used"], i * 2 * NB + NB)
                if i == 0:
                    link(V.tensor_copy(ranku[:, :], bt[0][:, 0:NB]))
                V.tensor_copy(rank[:, i, :], bt[0][:, 0:NB]).then_inc(S["ranked_sb"], 1)
                dve.wait_ge(S["ranked_sb"], i + 1)

            def fetch_places(i, out_col, done):
                dve.wait_ge(S["flags_used"], (i + 1) * 2 * NB)
                s5 = sorted5[:, i, :, :]
                V.tensor_copy(s5.rearrange("p b v -> p (b v)"), bt[1][:, 0:5 * NB]).then_inc(S["placed"], 1)
                dve.wait_ge(S["placed"], i + 1)
                link(V.scalar_tensor_tensor(rest[:, :], s5[:, :, 0], float(P), s5[:, :, 1], ALU.mult, ALU.add))
                V.tensor_scalar(perm[:, i, 0, :], rest[:, :], 2.0, None, ALU.mult)
                V.tensor_scalar(perm[:, i, 1, :], rest[:, :], 2.0, 1.0, ALU.mult, ALU.add)
                link(V.tensor_copy(perm[:, i, 2, :], rest[:, :]))
                link(V.tensor_tensor(rest[:, :], s5[:, :, 3], s5[:, :, 4], ALU.add))
                V.tensor_tensor(out_col[:, :], rest[:, :], s5[:, :, 2], ALU.add).then_inc(S[done], 1)
                dve.wait_ge(S[done], 1)

            dve.wait_ge(S["p_col"], 1)
            V.tensor_copy(rcol[:, :], bt[3][:, 0:W:W // NB]).then_inc(S["rcol_sb"], 1)
            dve.wait_ge(S["rcol_sb"], 1)
            dve.wait_ge(S["r_even"], 2)
            dve.wait_ge(S["r_odd"], 2)
            dve.wait_ge(S["ramp"], 1)
            values(0, rcol)
            for step in range(2 * NB):
                if step == NB:
                    fetch_ranks(0)
                sort_step(0, rrow, rcol, step)
            fetch_places(0, rs, "perm_r")
            link(V.tensor_reduce(sc[:, 7:8], rrow[:, :], AX.X, ALU.max))
            link(V.tensor_scalar(sc[:, 0:1], sc[:, 7:8], -1.0, None, ALU.mult))
            V.tensor_scalar(sc[:, 1:2], sc[:, 7:8], -SLOPE, None, ALU.mult).then_inc(S["m_ready"], 1)
            dve.wait_ge(S["row_c"], 1)
            dve.wait_ge(S["p_col"], 2)
            V.tensor_copy(ccol[:, :], bt[2][:, 0:W:W // NB]).then_inc(S["ccol_sb"], 1)
            dve.wait_ge(S["ccol_sb"], 1)
            values(1, ccol)
            dve.wait_ge(S["e_exp"], 2)
            dve.wait_ge(S["e_zero"], 1)
            Ef = [E[:, d, :, :].rearrange("p b r -> p (b r)") for d in range(2)]
            for d in range(2):
                for g in range(3):
                    for br in range(2):
                        o = 32 * g + NB * br
                        dst = Ef[d][:, o:o + (R + 1) * (NB - 1) + 1:R + 1]
                        if d == 0:
                            i = V.tensor_copy(dst, eexp[:, br, :])
                        else:
                            i = V.tensor_tensor(dst, eexp[:, br, :], Ef[0][:, o:o + (R + 1) * (NB - 1) + 1:R + 1], ALU.subtract)
                i.then_inc(S["e_ready"], 1)
                dve.wait_ge(S["e_ready"], d + 1)

            def staircase():
                dve.wait_ge(S["ends_in"], 32)
                dve.wait_ge(S["crow_sb"], 1)
                rmax, rmin = ends[:, 0, :], ends[:, 1, :]
                cmax, cmin = crow[:, 0:N:P], crow[:, P - 1:N:P]
                link(V.tensor_tensor(sc[:, 2:3], ends[:, 0, 0:1], crow[:, 0:1], ALU.add))
                link(V.scalar_tensor_tensor(sc[:, 3:4], sc[:, 2:3], SLOPE, sc[:, 2:3], ALU.mult, ALU.max))
                link(V.tensor_scalar(sc[:, 4:5], sc[:, 3:4], -1.0, None, ALU.mult))
                link(V.tensor_scalar(sc[:, 5:6], sc[:, 3:4], -1.0, DSCALE, ALU.mult, ALU.add))
                link(V.scalar_tensor_tensor(sc[:, 6:7], ends[:, 0, 0:1], cstt[:, 0:1], sc[:, 5:6], ALU.mult, ALU.add))
                jk3 = tmp[:, 0:NB * NB].rearrange("p (j k) -> p j k", j=NB)
                for o, (re, ce, op) in enumerate(((rmin, cmin, ALU.is_gt), (rmax, cmax, ALU.is_le))):
                    link(V.tensor_tensor(jk3, ce.unsqueeze(2).to_broadcast([P, NB, NB]), re.unsqueeze(1).to_broadcast([P, NB, NB]), ALU.add))
                    link(V.tensor_scalar(jk3, jk3, 0.0, None, op))
                    link(V.tensor_reduce(t16[:, o, :], jk3, AX.X, ALU.add))
                lo, hi = t16[:, 0, :], t16[:, 1, :]
                link(V.tensor_scalar(lo, lo, float(NB - 1), None, ALU.min))
                link(V.tensor_scalar(hi, hi, -1.0, float(NB - 1), ALU.mult, ALU.add))
                link(V.tensor_tensor(hi, hi, lo, ALU.max))
                link(V.tensor_copy(lohi[:, 0, :], lo))
                link(V.tensor_scalar(lohi[:, 1, :], hi, 1.0, None, ALU.add))
                link(V.tensor_scalar(t16[:, 2, :], lo, cstt[:, 2:3], None, ALU.mult))
                link(V.scalar_tensor_tensor(t16[:, 2, :], hi, cstt[:, 3:4], t16[:, 2, :], ALU.mult, ALU.add))
                V.tensor_scalar(mask[:, :], t16[:, 2, :], cstt[:, 1:2], None, ALU.is_gt).then_inc(S["mask_ready"], 1)
                dve.wait_ge(S["mask_ready"], 1)

            def staircase_slots():
                lo = t16[:, 0, :]
                link(V.tensor_tensor(t16[:, 2, :], cstt[:, 4:4 + NB], lo, ALU.subtract))
                s3 = tmp[:, 0:NS * NB].rearrange("p (s j) -> p s j", s=NS)
                ramp = cstt[:, 4 + NB:4 + NB + NS]
                link(V.tensor_tensor(s3, t16[:, 2, :].unsqueeze(1).to_broadcast([P, NS, NB]),
                                     ramp.unsqueeze(2).to_broadcast([P, NS, NB]), ALU.is_lt))
                link(V.tensor_reduce(steps[:, 0, :], s3, AX.X, ALU.add))
                link(V.tensor_scalar(steps[:, 0, :], steps[:, 0, :], float(NB - 1), None, ALU.min))
                link(V.tensor_tensor(steps[:, 1, :], steps[:, 0, :], ramp, ALU.subtract))
                link(V.tensor_scalar(steps[:, 1, :], steps[:, 1, :], float(NB - 1), 0.0, ALU.add, ALU.max))
                link(V.tensor_scalar(steps[:, 1, :], steps[:, 1, :], float(NB - 1), None, ALU.min))
                link(V.tensor_scalar(jk[:, :], steps[:, 0, :], float(P), None, ALU.mult))
                link(V.tensor_tensor(s3, steps[:, 1, :].unsqueeze(2).to_broadcast([P, NS, NB]),
                                     ramp[:, 0:NB].unsqueeze(1).to_broadcast([P, NS, NB]), ALU.is_equal))
                link(V.tensor_tensor(s3, s3, rs[:, :].unsqueeze(1).to_broadcast([P, NS, NB]), ALU.mult))
                V.tensor_reduce(rslot[:, :], s3, AX.X, ALU.add).then_inc(S["slots_ready"], 1)

            def leaky_relu(i):
                z, _, s1 = batch(i)
                dve.wait_ge(S["d_z"], s1)
                V.scalar_tensor_tensor(z, z, SLOPE, z, ALU.mult, ALU.max).then_inc(S["d_lz"], 1)

            def den_halves(i):
                z, (hi16, lo16), _ = batch(i)
                dve.wait_ge(S["d_exp"], i + 1)
                link(V.tensor_copy(hi16, z))
                V.tensor_tensor(lo16, z, hi16, ALU.subtract).then_inc(S["d_lo"], 1)

            for n in range(2 * NB):
                if n == NB // 2:
                    fetch_ranks(1)
                for step in c_steps(n):
                    sort_step(1, crow, ccol, step)
                if n == NB + 1:
                    fetch_places(1, cs, "perm_c")
                if n == STAIR:
                    staircase()
                if n == STAIR + 1:
                    staircase_slots()
                if n == STAIR + 3:
                    dve.wait_ge(S["w_hi"], 1)
                    V.tensor_tensor(wgt[64:R, :], tmp[64:R, :], wgt[64:R, :], ALU.subtract).then_inc(S["w_lo"], 1)
                for i in range(len(BATCH)):
                    if n == STAIR + 4 + 2 * i:
                        leaky_relu(i)
                    if n == STAIR + 5 + 2 * i:
                        den_halves(i)
                if n % LOS < LOS - 1:
                    b, h = divmod(n, 2)
                    dve.wait_ge(S["hi_done"], n + 1)
                    V.tensor_tensor(Alo[:, b, h * H:(h + 1) * H], st[n % NG], Ahi[:, b, h * H:(h + 1) * H],
                                    ALU.subtract).then_inc(S["lo_dve"], 1)

            for c in range(NC):
                dve.wait_ge(S["sums_hi"], c + 1)
                V.tensor_tensor(sums[32:64, c * W:(c + 1) * W], ps[32:64, c, :], sums[32:64, c * W:(c + 1) * W],
                                ALU.subtract).then_inc(S["sums_sb"], 1)

            def att_of(t, c, first):
                dve.wait_ge(S["exp_done"], t + 1)
                if not first:
                    dve.wait_ge(S["bt_added"], t - NC + 1)
                V.scalar_tensor_tensor(att[c], num[c], 1.0 / 256, L_t[c], ALU.mult, ALU.mult).then_inc(S["att_ready"], 1)

            def pair(J0, first):
                for u in range(2):
                    J = J0 + u
                    for c in range(NC):
                        t = J * NC + c
                        dve.wait_ge(S["q_ready"], t + 1)
                        if not (first and u == 0 and c < 2):
                            dve.wait_ge(S["sub_done"], t - 1)
                        V.scalar_tensor_tensor(lz_t[c % 2], q_t[c % 2], SLOPE, q_t[c % 2], ALU.mult, ALU.max).then_inc(S["lz_ready"], 1)
                        dve.wait_ge(S["lz_ready"], t + 1)
                        dve.wait_ge(S["ln_done"], t + 1)
                        V.tensor_tensor(L_t[c], lz_t[c % 2], L_t[c], ALU.subtract).then_inc(S["sub_done"], 1)
                        if not (first and u == 0 and c == 0):
                            att_of(t - 1, (c - 1) % NC, first and (u == 0 or c == 0))

            pair(0, True)
            with dve.Fori(1, NP2) as p:
                pair(2 * p, False)
            att_of(NB * NC - 1, NC - 1, False)

            for g in range(2):
                dve.wait_ge(S["bhi_done"], g + 1)
                gb = slice(g * NB // 2, (g + 1) * NB // 2)
                V.tensor_tensor(B16[:, 1, gb, :].rearrange("p b f -> p (b f)"), Bs[:, g * N // 2:(g + 1) * N // 2],
                                B16[:, 0, gb, :].rearrange("p b f -> p (b f)"), ALU.subtract).then_inc(S["blo_done"], 1)
            dve.wait_ge(S["x_in"], 16)
            dve.wait_ge(S["b_out"], 16 * NB)
            for c in range(NC):
                dve.wait_ge(S["h_t"], c + 1)
                blocks = range(4 * c, 4 * c + 4)
                yc = y[:, 4 * c:4 * c + 4, :].rearrange("p b f -> p (b f)")
                link(V.tensor_tensor(yc, xs[:, c * W:(c + 1) * W], num[c], ALU.add))
                for b in blocks:
                    i = V.bn_stats(stats[:, b, :], y[:, b, :])
                link(i)
                for b in blocks:
                    i = V.bn_aggr(mv[:, b, :], stats[:, b, :])
                i.then_inc(S["var"], 1)
                dve.wait_ge(S["std"], c + 1)
                link(V.reciprocal(rstd[:, 4 * c:4 * c + 4], rstd[:, 4 * c:4 * c + 4]))
                for b in blocks:
                    i = V.tensor_scalar(y[:, b, :], y[:, b, :], mv[:, b, 0:1], rstd[:, b:b + 1], ALU.subtract, ALU.mult)
                i.then_inc(S["y_ready"], 1)


def kernel(x, adj, L0_gnn_W, L0_gnn_a):
    import concourse.bacc as bacc
    from concourse.bass_utils import run_bass_kernel_spmd

    x, w, a = np.asarray(x), np.asarray(L0_gnn_W), np.asarray(L0_gnn_a)
    cst, before, ids = constants()
    arrays = {
        "xT": np.ascontiguousarray(x.T),
        "x": np.ascontiguousarray(x),
        "adjT": np.ascontiguousarray(np.asarray(adj).T),
        "w": np.ascontiguousarray(w),
        "wT": np.ascontiguousarray(w.T),
        "a2": np.ascontiguousarray(a.reshape(2, FEAT).T),
        "cst": np.ascontiguousarray(cst),
        "before": before,
        "ids": np.ascontiguousarray(ids),
    }
    nc = bacc.Bacc("TRN2", target_bir_lowering=False, num_devices=1)
    args = [nc.dram_tensor(n, v.shape, mybir.dt.from_np(v.dtype), kind="ExternalInput").ap() for n, v in arrays.items()]
    args.append(nc.dram_tensor("out", x.shape, mybir.dt.float32, kind="ExternalOutput").ap())
    graph_attention_layernorm(nc, *args)
    r = run_bass_kernel_spmd(nc, [arrays], core_ids=[0])
    return r.results[0]["out"]
```
